# Optimizing a Trainium2 kernel written in Bass

```python
import numpy as np
import jax
import jax.numpy as jnp

def _softmax(x, axis=-1):
    return jax.nn.softmax(x, axis=axis)

def _gelu(x):
    return jax.nn.gelu(x, approximate=True)

def _silu(x):
    return jax.nn.silu(x)

def _sigmoid(x):
    return jax.nn.sigmoid(x)

def _layernorm(x, axis=-1, eps=1e-05):
    m = jnp.mean(x, axis=axis, keepdims=True)
    v = jnp.var(x, axis=axis, keepdims=True)
    return (x - m) / jnp.sqrt(v + eps)

def _scatter_add(tgt, idx, src, axis=0):
    return tgt.at[idx].add(src)

def _segment_sum(src, seg, n):
    return jax.ops.segment_sum(src, seg, n)
kernel_name = 'mk_vit_tower_postln_d1_tok_img768_r4_59afe6'

def setup_inputs(seed: int=0):
    np.random.seed(seed)
    _w = jnp.asarray

    def _rec_inputs():
        import jax
        import jax.numpy as jnp
        _rk = jax.random.key(seed)
        x = -0.000222058 + 0.999998 * jax.random.normal(jax.random.fold_in(_rk, 1), (4, 3, 128, 128), jnp.float32)
        return x
    x = _rec_inputs()

    def _L0_tok_setup():
        import jax, jax.numpy as jnp
        import numpy as np
        key = jax.random.key(seed)
        kx, kw, kb = jax.random.split(key, 3)
        B, C, H, Wd = (32, 3, 128, 128)
        P, E = (16, 192)
        x = jax.random.normal(kx, (B, C, H, Wd), dtype=jnp.float32)
        W = jax.random.normal(kw, (P * P, E), dtype=jnp.float32) * 0.02
        b = jax.random.normal(kb, (E,), dtype=jnp.float32) * 0.02
        return {'x': x, 'W': W, 'b': b}
    _L0_tok_all = _L0_tok_setup()
    _L0_tok_in = {k: v for k, v in _L0_tok_all.items() if k in ('W', 'b')}
    del _L0_tok_all

    def _L0_attn_setup():
        import jax, jax.numpy as jnp
        import numpy as np
        D_MODEL = 192
        EXPAND = 2
        D_INNER = EXPAND * D_MODEL
        D_STATE = 64
        D_CONV = 4
        DT_RANK = (D_MODEL + 15) // 16
        BATCH = 8
        SEQ = 1024
        LN_EPS = 1e-05

        def _mamba_block(x, ln_w, ln_b, in_proj_w, conv_w, conv_b, x_proj_w, dt_proj_w, dt_proj_b, A_log, D, out_proj_w):
            mu = jnp.mean(x, axis=-1, keepdims=True)
            var = jnp.mean(jnp.square(x - mu), axis=-1, keepdims=True)
            xn = (x - mu) * jax.lax.rsqrt(var + LN_EPS) * ln_w + ln_b
            xz = jnp.einsum('bld,ed->ble', xn, in_proj_w)
            xc, z = jnp.split(xz, 2, axis=-1)
            xt = jnp.transpose(xc, (0, 2, 1))
            xconv = jax.lax.conv_general_dilated(xt, conv_w, window_strides=(1,), padding=[(D_CONV - 1, 0)], dimension_numbers=('NCH', 'OIH', 'NCH'), feature_group_count=D_INNER)
            xs = jax.nn.silu(jnp.transpose(xconv, (0, 2, 1)) + conv_b)
            dbl = jnp.einsum('bld,ed->ble', xs, x_proj_w)
            dtp, Bm, Cm = jnp.split(dbl, [DT_RANK, DT_RANK + D_STATE], axis=-1)
            dt = jax.nn.softplus(jnp.einsum('blr,dr->bld', dtp, dt_proj_w) + dt_proj_b)
            A = -jnp.exp(A_log)

            def step(h, inp):
                dt_t, B_t, C_t, x_t = inp
                dA = jnp.exp(dt_t[:, :, None] * A)
                h = dA * h + dt_t[:, :, None] * B_t[:, None, :] * x_t[:, :, None]
                y_t = jnp.einsum('bdn,bn->bd', h, C_t)
                return (h, y_t)
            h0 = jnp.zeros((x.shape[0], D_INNER, D_STATE), xs.dtype)
            seq_in = (jnp.transpose(dt, (1, 0, 2)), jnp.transpose(Bm, (1, 0, 2)), jnp.transpose(Cm, (1, 0, 2)), jnp.transpose(xs, (1, 0, 2)))
            _, ys = jax.lax.scan(step, h0, seq_in)
            y = jnp.transpose(ys, (1, 0, 2)) + xs * D
            y = y * jax.nn.silu(z)
            out = jnp.einsum('bld,ed->ble', y, out_proj_w)
            return x + out
        key = jax.random.key(seed)
        ks = jax.random.split(key, 8)
        s = 0.02
        x = jax.random.normal(ks[0], (BATCH, SEQ, D_MODEL), jnp.float32)
        ln_w = jnp.ones((D_MODEL,), jnp.float32)
        ln_b = jnp.zeros((D_MODEL,), jnp.float32)
        in_proj_w = jax.random.normal(ks[1], (2 * D_INNER, D_MODEL), jnp.float32) * s
        conv_w = jax.random.normal(ks[2], (D_INNER, 1, D_CONV), jnp.float32) * 0.1
        conv_b = jnp.zeros((D_INNER,), jnp.float32)
        x_proj_w = jax.random.normal(ks[3], (DT_RANK + 2 * D_STATE, D_INNER), jnp.float32) * s
        dt_proj_w = jax.random.normal(ks[4], (D_INNER, DT_RANK), jnp.float32) * DT_RANK ** (-0.5)
        dt_init = jax.random.uniform(ks[5], (D_INNER,), jnp.float32) * (0.1 - 0.001) + 0.001
        dt_proj_b = jnp.log(jnp.expm1(dt_init))
        A_log = jnp.log(jnp.broadcast_to(jnp.arange(1, D_STATE + 1, dtype=jnp.float32), (D_INNER, D_STATE)))
        D = jnp.ones((D_INNER,), jnp.float32)
        out_proj_w = jax.random.normal(ks[6], (D_MODEL, D_INNER), jnp.float32) * s
        return {'x': x, 'ln_w': ln_w, 'ln_b': ln_b, 'in_proj_w': in_proj_w, 'conv_w': conv_w, 'conv_b': conv_b, 'x_proj_w': x_proj_w, 'dt_proj_w': dt_proj_w, 'dt_proj_b': dt_proj_b, 'A_log': A_log, 'D': D, 'out_proj_w': out_proj_w}
    _L0_attn_all = _L0_attn_setup()
    _L0_attn_in = {k: v for k, v in _L0_attn_all.items() if k in ('ln_w', 'ln_b', 'in_proj_w', 'conv_w', 'conv_b', 'x_proj_w', 'dt_proj_w', 'dt_proj_b', 'A_log', 'D', 'out_proj_w')}
    del _L0_attn_all

    def _L0_ffn_setup():
        import jax, jax.numpy as jnp
        import numpy as np
        from jax import lax
        B, T, H = (2, 256, 192)
        E = 64
        I = 64
        TOP_K = 8
        key = jax.random.key(seed)
        k0, k1, k2, k3, k4 = jax.random.split(key, 5)
        hidden_states = jax.random.normal(k0, (B, T, H), dtype=jnp.float32)
        router_w = jax.random.normal(k1, (E, H), dtype=jnp.float32) * 0.02
        w_gate = jax.random.normal(k2, (E, H, I), dtype=jnp.float32) * 0.02
        w_up = jax.random.normal(k3, (E, H, I), dtype=jnp.float32) * 0.02
        w_down = jax.random.normal(k4, (E, I, H), dtype=jnp.float32) * 0.02
        return {'hidden_states': hidden_states, 'router_w': router_w, 'w_gate': w_gate, 'w_up': w_up, 'w_down': w_down}
    _L0_ffn_all = _L0_ffn_setup()
    _L0_ffn_in = {k: v for k, v in _L0_ffn_all.items() if k in ('router_w', 'w_gate', 'w_up', 'w_down')}
    del _L0_ffn_all
    return {'x': x, 'L0_tok_W': _L0_tok_in['W'], 'L0_tok_b': _L0_tok_in['b'], 'L0_attn_ln_w': _L0_attn_in['ln_w'], 'L0_attn_ln_b': _L0_attn_in['ln_b'], 'L0_attn_in_proj_w': _L0_attn_in['in_proj_w'], 'L0_attn_conv_w': _L0_attn_in['conv_w'], 'L0_attn_conv_b': _L0_attn_in['conv_b'], 'L0_attn_x_proj_w': _L0_attn_in['x_proj_w'], 'L0_attn_dt_proj_w': _L0_attn_in['dt_proj_w'], 'L0_attn_dt_proj_b': _L0_attn_in['dt_proj_b'], 'L0_attn_A_log': _L0_attn_in['A_log'], 'L0_attn_D': _L0_attn_in['D'], 'L0_attn_out_proj_w': _L0_attn_in['out_proj_w'], 'L0_ffn_router_w': _L0_ffn_in['router_w'], 'L0_ffn_w_gate': _L0_ffn_in['w_gate'], 'L0_ffn_w_up': _L0_ffn_in['w_up'], 'L0_ffn_w_down': _L0_ffn_in['w_down']}

def reference(x, L0_tok_W, L0_tok_b, L0_attn_ln_w, L0_attn_ln_b, L0_attn_in_proj_w, L0_attn_conv_w, L0_attn_conv_b, L0_attn_x_proj_w, L0_attn_dt_proj_w, L0_attn_dt_proj_b, L0_attn_A_log, L0_attn_D, L0_attn_out_proj_w, L0_ffn_router_w, L0_ffn_w_gate, L0_ffn_w_up, L0_ffn_w_down):
    import jax
    import jax.numpy as jnp

    def _L0_tok_ref(x, W, b):
        import jax, jax.numpy as jnp
        import numpy as np
        B, C, H, Wd = x.shape
        P = int(np.sqrt(W.shape[0]))
        Hp, Wp = (H // P, Wd // P)
        patches = x.reshape(B, C, Hp, P, Wp, P).transpose(0, 1, 2, 4, 3, 5)
        patches = patches.reshape(B, C * Hp * Wp, P * P)
        return jnp.einsum('bnp,pe->bne', patches, W) + b

    def _L0_attn_ref(x, ln_w, ln_b, in_proj_w, conv_w, conv_b, x_proj_w, dt_proj_w, dt_proj_b, A_log, D, out_proj_w):
        import jax, jax.numpy as jnp
        import numpy as np
        D_MODEL = 192
        EXPAND = 2
        D_INNER = EXPAND * D_MODEL
        D_STATE = 64
        D_CONV = 4
        DT_RANK = (D_MODEL + 15) // 16
        BATCH = 8
        SEQ = 1024
        LN_EPS = 1e-05

        def _mamba_block(x, ln_w, ln_b, in_proj_w, conv_w, conv_b, x_proj_w, dt_proj_w, dt_proj_b, A_log, D, out_proj_w):
            mu = jnp.mean(x, axis=-1, keepdims=True)
            var = jnp.mean(jnp.square(x - mu), axis=-1, keepdims=True)
            xn = (x - mu) * jax.lax.rsqrt(var + LN_EPS) * ln_w + ln_b
            xz = jnp.einsum('bld,ed->ble', xn, in_proj_w)
            xc, z = jnp.split(xz, 2, axis=-1)
            xt = jnp.transpose(xc, (0, 2, 1))
            xconv = jax.lax.conv_general_dilated(xt, conv_w, window_strides=(1,), padding=[(D_CONV - 1, 0)], dimension_numbers=('NCH', 'OIH', 'NCH'), feature_group_count=D_INNER)
            xs = jax.nn.silu(jnp.transpose(xconv, (0, 2, 1)) + conv_b)
            dbl = jnp.einsum('bld,ed->ble', xs, x_proj_w)
            dtp, Bm, Cm = jnp.split(dbl, [DT_RANK, DT_RANK + D_STATE], axis=-1)
            dt = jax.nn.softplus(jnp.einsum('blr,dr->bld', dtp, dt_proj_w) + dt_proj_b)
            A = -jnp.exp(A_log)

            def step(h, inp):
                dt_t, B_t, C_t, x_t = inp
                dA = jnp.exp(dt_t[:, :, None] * A)
                h = dA * h + dt_t[:, :, None] * B_t[:, None, :] * x_t[:, :, None]
                y_t = jnp.einsum('bdn,bn->bd', h, C_t)
                return (h, y_t)
            h0 = jnp.zeros((x.shape[0], D_INNER, D_STATE), xs.dtype)
            seq_in = (jnp.transpose(dt, (1, 0, 2)), jnp.transpose(Bm, (1, 0, 2)), jnp.transpose(Cm, (1, 0, 2)), jnp.transpose(xs, (1, 0, 2)))
            _, ys = jax.lax.scan(step, h0, seq_in)
            y = jnp.transpose(ys, (1, 0, 2)) + xs * D
            y = y * jax.nn.silu(z)
            out = jnp.einsum('bld,ed->ble', y, out_proj_w)
            return x + out
        return _mamba_block(x, ln_w, ln_b, in_proj_w, conv_w, conv_b, x_proj_w, dt_proj_w, dt_proj_b, A_log, D, out_proj_w)

    def _L0_ffn_ref(hidden_states, router_w, w_gate, w_up, w_down):
        import jax, jax.numpy as jnp
        import numpy as np
        from jax import lax
        B, T, H = (2, 256, 192)
        E = 64
        I = 64
        TOP_K = 8
        b, t, h = hidden_states.shape
        x = hidden_states.reshape(-1, h)
        n = x.shape[0]
        logits = x @ router_w.T
        probs = jax.nn.softmax(logits.astype(jnp.float32), axis=-1)
        top_w, top_i = lax.top_k(probs, TOP_K)
        top_w = top_w / jnp.sum(top_w, axis=-1, keepdims=True)
        top_w = top_w.astype(x.dtype)
        rw = jnp.zeros((n, E), dtype=x.dtype).at[jnp.arange(n)[:, None], top_i].set(top_w)

        def step(acc, inp):
            wg, wu, wd, w = inp
            hmid = jax.nn.silu(x @ wg) * (x @ wu)
            return (acc + w[:, None] * (hmid @ wd), None)
        out, _ = lax.scan(step, jnp.zeros_like(x), (w_gate, w_up, w_down, rw.T))
        return out.reshape(b, t, h)
    h = _L0_tok_ref(x, L0_tok_W, L0_tok_b)
    h = _layernorm(h + _L0_attn_ref(h, L0_attn_ln_w, L0_attn_ln_b, L0_attn_in_proj_w, L0_attn_conv_w, L0_attn_conv_b, L0_attn_x_proj_w, L0_attn_dt_proj_w, L0_attn_dt_proj_b, L0_attn_A_log, L0_attn_D, L0_attn_out_proj_w), axis=-1)
    h = _layernorm(h + _L0_ffn_ref(h, L0_ffn_router_w, L0_ffn_w_gate, L0_ffn_w_up, L0_ffn_w_down), axis=-1)
    return h

_drawn_inputs = setup_inputs


def setup_inputs(seed=0):
    import zlib

    import numpy as np

    out = dict(_drawn_inputs(seed))
    spreads = {'L0_attn_ln_w': (1.0, 0.6),
     'L0_attn_ln_b': (0.0, 0.8),
     'L0_attn_conv_b': (0.0, 0.8),
     'L0_attn_D': (1.0, 0.6)}
    factors = {'L0_attn_in_proj_w': 8.0,
     'L0_attn_conv_w': 8.0,
     'L0_attn_x_proj_w': 8.0,
     'L0_attn_dt_proj_w': 8.0,
     'L0_attn_dt_proj_b': 8.0,
     'L0_attn_A_log': 8.0,
     'L0_attn_out_proj_w': 8.0,
     'L0_ffn_router_w': 8.0,
     'L0_ffn_w_gate': 8.0,
     'L0_ffn_w_up': 8.0,
     'L0_ffn_w_down': 8.0}
    for name, (base, spread) in spreads.items():
        noise = np.random.default_rng([zlib.crc32(name.encode()), seed]).standard_normal(out[name].shape)
        drawn = base * np.exp(spread * noise) if base else spread * noise
        out[name] = jnp.asarray(drawn.astype(out[name].dtype))
    for name, factor in factors.items():
        out[name] = (out[name] * factor).astype(out[name].dtype)
    return out
```

```python
from contextlib import ExitStack

import concourse.bass as bass
from concourse import mybir

F32 = mybir.dt.float32
BF16 = mybir.dt.bfloat16
ALU = mybir.AluOpType
ACT = mybir.ActivationFunctionType

NB = 4
T = 192
TT = 96
E = 192
EK = 96
NC = 3
N = 64
R = 12
CONV = 4
PAIRS = 32
HALF = 32
ROUNDS = 16
SUB = 6
EPS = 1e-5




def log1p_coefficients():
    import numpy as np
    deg = 11
    x = 0.5 + 0.5 * np.cos(np.pi * (np.arange(deg + 1) + 0.5) / (deg + 1))
    y = np.log1p(x) / x
    cheb = np.polynomial.Chebyshev.fit(x, y, deg, domain=[0, 1])
    return [float(c) for c in cheb.convert(kind=np.polynomial.Polynomial).coef]


def vit_mamba_moe(nc, x, tok_w, tok_b, ln_w, ln_b, in_w, conv_w, conv_b, xp_w, dtp_w, dtp_b, a_log, d_skip, out_w,
                  router_w, wgu, wd, ident, eye3, out):
    with ExitStack() as ctx:
        def sb(name, shape, dt=F32):
            return ctx.enter_context(nc.sbuf_tensor(name, shape, dt))

        def bank(name, dt=F32):
            return ctx.enter_context(nc.psum_tensor(name, [128, 512], dt))

        def sem(name):
            return ctx.enter_context(nc.semaphore(name))

        tokw = sb("tokw", [128, 2, E])
        tokb = sb("tokb", [1, E])
        ones = sb("ones", [1, TT])
        lnw = sb("lnw", [EK, 2])
        lnb = sb("lnb", [EK, 2])
        inw = sb("inw", [EK, 2, 2 * NC * 128])
        convw = sb("convw", [128, NC, CONV])
        convb = sb("convb", [128, NC])
        xpw = sb("xpw", [128, NC, R + 4 * 96])
        dtw = sb("dtw", [R, NC * 128])
        dtb = sb("dtb", [128, NC])
        alog = sb("alog", [128, NC, N])
        aneg = sb("aneg", [128, NC, N])
        dsk = sb("dsk", [128, NC])
        outw = sb("outw", [128, NC, E])
        rw_w = sb("rw_w", [EK, 2, 64])
        idn = sb("idn", [128, 128])
        eye = sb("eye", [96, HALF])
        sel_state = sb("sel_state", [96, HALF, 128], BF16)
        sel_expert = sb("sel_expert", [96, HALF, 64], BF16)
        zero_w = sb("zero_w", [1, 128], BF16)
        zero_x = sb("zero_x", [1, 2 * T], BF16)

        xb = sb("xb", [128, 2, T])
        h = sb("h", [TT, 2, E])
        stats = sb("stats", [TT, 2, 6])
        mv = sb("mv", [TT, 2, 2])
        var = sb("var", [TT, 2])
        root = sb("root", [TT, 2])
        newton = sb("newton", [TT, 2])
        rstd = sb("rstd", [TT, 2])
        hn = sb("hn", [TT, 2, E])
        hnT = sb("hnT", [EK, 2, T])
        xpad = sb("xpad", [128, NC, CONV - 1 + T])
        zth = sb("zth", [128, NC, T])
        gate = sb("gate", [128, NC, T])
        cacc = sb("cacc", [128, NC, T])
        cth = sb("cth", [128, NC, T])
        xs = sb("xs", [128, NC, T])
        dtr = sb("dtr", [R, T])
        vabs = sb("vabs", [128, NC, T])
        vexp = sb("vexp", [128, NC, T])
        vmax = sb("vmax", [128, NC, T])
        poly = sb("poly", [128, NC, T])
        dt = sb("dt", [128, NC, T])
        u = sb("u", [128, NC, T])
        bc_split = sb("bc_split", [96, 2, 2, T], BF16)
        bc_rest = sb("bc_rest", [96, 2, 2, T])
        yt = sb("yt", [128, NC, T])
        yg = sb("yg", [128, NC, T])
        res = sb("res", [TT, 2, E])
        h1 = sb("h1", [TT, 2, E])
        h1T = sb("h1T", [EK, 2, T])
        logit = sb("logit", [TT, 2, 64])
        top8 = sb("top8", [TT, 2, 8])
        nmax = sb("nmax", [TT, 2])
        lrest = sb("lrest", [TT, 2, 64])
        lexp = sb("lexp", [TT, 2, 64])
        lmask = sb("lmask", [TT, 2, 64])
        wsum = sb("wsum", [TT, 2])
        winv = sb("winv", [TT, 2])
        wrep = sb("wrep", [TT, 2, 2, 3, HALF])
        rw_split = sb("rw_split", [96, 2, T], BF16)
        rw_rest = sb("rw_rest", [96, 2, T])
        ores = sb("ores", [TT, 2, E])
        outb = sb("outb", [TT, 2, E])

        da = sb("da", [128, SUB, 2, T])
        hs = sb("hs", [128, SUB, 2, T])
        hc = sb("hc", [128, SUB, 2, T])
        cbc = sb("cbc", [128, 2, 2, T])
        gu_w = sb("gu_w", [EK, 2, 2, 2, 128])
        dn_w = sb("dn_w", [128, 2, E])
        rwb = sb("rwb", [128, 2, T])
        gth = sb("gth", [128, 2, T])
        hm1 = sb("hm1", [128, 2, T])
        hm2 = sb("hm2", [128, 2, T])
        hm = sb("hm", [128, 2, T])

        pD = ctx.enter_context(nc.psum_tensor("pD", [128, 2, 512], F32))
        pB = bank("pB")
        pC = bank("pC")
        pY = ctx.enter_context(nc.psum_tensor("pY", [128, 2, 512], F32))
        pG = bank("pG")
        pM = bank("pM")

        def y_of(c):
            return pY[:, c // 2, (c % 2) * T:(c % 2) * T + T]

        def pair(ap, w=T):
            return ap[:, 0:2 * w].rearrange("p (a t) -> p a t", a=2)

        names = """w_in x_in zeros_set ones_set pad_set da_reset a_exp a_ready sel_ready embed_done h_copied hn_ready hnT_done
            hnT_ready in_done xc_copied z_tanh gate_ready z_copied conv_ready conv_tanh xs_ready xp_done dtr_ready bc_ready dtp_done
            vabs_ready vexp_ready vmax_ready u_ready y_zeroed b_filled c_filled c_copied dbx_done da_ready scan_done
            hc_done y_added y_taken yg_ready op_done h1_ready h1T_done h1T_ready rt_done logit_ready nmax_ready lexp_ready
            wrep_ready wT_done rw_ready m_zeroed gu_loaded0 gu_loaded1 dn_loaded0 dn_loaded1 gu_done dn_done rw_filled rw_copied g_tanh hm2_done
            hm_ready out_ready stored settled var_front root_front var_tail root_tail var_finish root_finish front_v tail_v hm1_done finish_v""".split()
        s = {n: sem(n) for n in names}

        WEIGHTS = [(tokw, tok_w), (tokb, tok_b), (idn, ident), (eye, eye3), (lnw, ln_w), (lnb, ln_b), (inw, in_w),
                   (convw, conv_w), (convb, conv_b), (xpw, xp_w), (dtw, dtp_w), (dtb, dtp_b), (alog, a_log),
                   (dsk, d_skip), (outw, out_w), (rw_w, router_w)]
        W_ALL = 16 * len(WEIGHTS)
        out_v = out.rearrange("b (t p) e -> p (b t) e", t=2)

        DBX0, SCAN0, HC0, YA0, CC0, RC0, GU0, DN0, HM20, HM0 = 3, SUB, SUB, SUB, 1, 1, 2, 2, 1, 2

        block = ctx.enter_context(nc.Block())

        @block.sync
        def _(sp):
            sp.dma_start(xb[:, :, :], x[0]).then_inc(s["x_in"], 16)
            for dst, src in WEIGHTS:
                sp.dma_start(dst[tuple(slice(None) for _ in dst.shape)], src).then_inc(s["w_in"], 16)

            def load_x(b):
                sp.wait_ge(s["embed_done"], b)
                sp.dma_start(xb[:, :, :].rearrange("p k t -> p (k t)"),
                             x.rearrange("b p k t -> p b (k t)")[:, bass.ds(b, 1), :]).then_inc(s["x_in"], 16)

            def load_experts(b):
                with sp.Fori(0, ROUNDS) as i:
                    for j in range(2):
                        sp.wait_ge(s["gu_done"], b * PAIRS + i * 2 + (j + 1))
                        sp.dma_start(gu_w[:, j].rearrange("p k g c -> p (k g c)"),
                                     wgu[:, bass.ds(i * 2 + j, 1), :]).then_inc(s[f"gu_loaded{j}"], 16)
                        sp.wait_ge(s["dn_done"], b * PAIRS + i * 2 + (j + 1))
                        sp.dma_start(dn_w[:, j, :], wd[:, bass.ds(i * 2 + j, 1), :]).then_inc(s[f"dn_loaded{j}"], 16)

            def store(b):
                sp.wait_ge(s["out_ready"], b * 2 + 2)
                sp.dma_start(out_v[:, bass.ds(b * 2, 2), :], outb[:, :, :]).then_inc(s["stored"], 16)

            load_experts(0)
            load_x(1)
            store(0)
            with sp.Fori(1, NB - 1) as b:
                load_experts(b)
                load_x(b + 1)
                store(b)
            load_experts(NB - 1)
            store(NB - 1)
            sp.wait_ge(s["stored"], 16 * NB)

        @block.tensor
        def _(pe):
            def front(b):
                pe.wait_ge(s["x_in"], b * 16 + 16)
                if not isinstance(b, int):
                    pe.wait_ge(s["h1_ready"], b)
                for t in range(2):
                    o = pD[0:TT, 0, t * E:(t + 1) * E]
                    for k in range(2):
                        pe.matmul(o, xb[:, k, t * TT:(t + 1) * TT], tokw[:, k, :], start=(k == 0), stop=False)
                    mm = pe.matmul(o, ones[0:1, :], tokb[0:1, :], start=False, stop=True)
                mm.then_inc(s["embed_done"], 1)
                pe.wait_ge(s["hn_ready"], b * 2 + 2)
                if not isinstance(b, int):
                    pe.wait_ge(s["h1T_ready"], b)
                for k in range(2):
                    for t in range(2):
                        mm = pe.transpose(pD[0:EK, 1, k * T + t * TT:k * T + (t + 1) * TT],
                                          hn[:, t, k * EK:(k + 1) * EK], idn[0:TT, 0:TT])
                mm.then_inc(s["hnT_done"], 1)
                pe.wait_ge(s["hnT_ready"], b * 2 + 2)
                if not isinstance(b, int):
                    pe.wait_ge(s["rw_ready"], b)
                    pe.wait_ge(s["rw_copied"], RC0 + b * ROUNDS)
                for m in range(6):
                    o = [pB, pC, pD[:, 0, :]][m // 2][:, (m % 2) * T:(m % 2) * T + T]
                    for k in range(2):
                        mm = pe.matmul(o, inw[:, k, m * 128:(m + 1) * 128], hnT[:, k, :], start=(k == 0), stop=(k == 1))
                    if m % 2:
                        mm.then_inc(s["in_done"], 1)
                pe.wait_ge(s["xs_ready"], b + 1)
                pe.wait_ge(s["xc_copied"], b * 3 + 3)
                pe.wait_ge(s["gate_ready"], b * 3 + 3)
                pe.wait_ge(s["z_tanh"], b * 2 + 2)
                for c in range(NC):
                    mm = pe.matmul(pD[0:R, 1, 0:T], xpw[:, c, 0:R], xs[:, c, :], start=(c == 0), stop=(c == 2))
                mm.then_inc(s["xp_done"], 1)
                for q in range(4):
                    o = [pB, pC][q // 2][0:96, (q % 2) * T:(q % 2) * T + T]
                    for c in range(NC):
                        mm = pe.matmul(o, xpw[:, c, R + q * 96:R + (q + 1) * 96], xs[:, c, :],
                                       start=(c == 0), stop=(c == 2))
                    if q % 2:
                        mm.then_inc(s["xp_done"], 1)
                pe.wait_ge(s["dtr_ready"], b + 1)
                for c in range(NC):
                    o = pD[:, c // 2, (c % 2) * T:(c % 2) * T + T]
                    mm = pe.matmul(o, dtw[:, c * 128:(c + 1) * 128], dtr[:, :], start=True, stop=True)
                mm.then_inc(s["dtp_done"], 1)

            def zero_y(b):
                if not isinstance(b, int):
                    pe.wait_ge(s["y_taken"], b * 3)
                for k in range(2):
                    mm = pe.matmul(pY[:, k, 0:2 * T], zero_w[:, :], zero_x[:, :], start=True, stop=True)

            def fill(b, i, j):
                k = b * PAIRS + i * 2 + j
                for which, bank_, filled in ((0, pB, "b_filled"), (1, pC, "c_filled")):
                    if which == 0:
                        pe.wait_ge(s["dbx_done"], DBX0 + k * 3)
                    else:
                        pe.wait_ge(s["c_copied"], CC0 + k)
                    for e in range(2):
                        n = i * 4 + j * 2 + e
                        mm = pe.matmul(bank_[:, e * T:(e + 1) * T], sel_state[:, bass.ds(n % HALF, 1), :].rearrange("p a m -> p (a m)"),
                                       bc_split[:, which, bass.ds(n // HALF, 1), :].rearrange("p a t -> p (a t)"), start=True, stop=True)
                    mm.then_inc(s[filled], 1)

            def add_y(b, i, j):
                for c in range(NC):
                    v = b * (ROUNDS * SUB) + i * SUB + (j * 3 + c)
                    pe.wait_ge(s["hc_done"], HC0 + 1 + v)
                    for e in range(2):
                        mm = pe.matmul(y_of(c), idn[:, :], hc[:, j * 3 + c, e, :], start=False, stop=False,
                                       skip_group_check=True)
                    mm.then_inc(s["y_added"], 1)

            def scan(b):
                zero_y(b)
                pe.wait_ge(s["bc_ready"], b * 2 + 2)
                for j in range(2):
                    fill(b, 0, j)
                with pe.Fori(0, ROUNDS - 1) as i:
                    for j in range(2):
                        fill(b, i + 1, j)
                        add_y(b, i, j)
                for j in range(2):
                    add_y(b, ROUNDS - 1, j)

            def tail(b):
                pe.wait_ge(s["yg_ready"], b + 1)
                for t in range(2):
                    for c in range(NC):
                        mm = pe.matmul(pD[0:TT, 0, t * E:(t + 1) * E], yg[:, c, t * TT:(t + 1) * TT], outw[:, c, :],
                                       start=(c == 0), stop=(c == 2))
                mm.then_inc(s["op_done"], 1)
                pe.wait_ge(s["h1_ready"], b + 1)
                for k in range(2):
                    for t in range(2):
                        mm = pe.transpose(pD[0:EK, 1, k * T + t * TT:k * T + (t + 1) * TT],
                                          h1[:, t, k * EK:(k + 1) * EK], idn[0:TT, 0:TT])
                mm.then_inc(s["h1T_done"], 1)
                pe.wait_ge(s["h1T_ready"], b + 1)
                for t in range(2):
                    for k in range(2):
                        mm = pe.matmul(pB[0:TT, t * 64:(t + 1) * 64], h1T[:, k, t * TT:(t + 1) * TT], rw_w[:, k, :],
                                       start=(k == 0), stop=(k == 1))
                mm.then_inc(s["rt_done"], 1)
                pe.wait_ge(s["wrep_ready"], b * 2 + 2)
                for hf in range(2):
                    for t in range(2):
                        mm = pe.transpose(pC[0:96, hf * T + t * TT:hf * T + (t + 1) * TT],
                                          wrep[:, t, hf].rearrange("p s e -> p (s e)"), idn[0:TT, 0:TT])
                mm.then_inc(s["wT_done"], 1)

            def zero_moe(b):
                if not isinstance(b, int):
                    pe.wait_ge(s["out_ready"], b * 2)
                pe.matmul(pM[0:TT, 0:2 * E], zero_w[:, 0:TT], zero_x[:, :], start=True, stop=True)

            def expert_weights(b, i):
                pe.wait_ge(s["rw_ready"], b + 1)
                pe.wait_ge(s["rw_copied"], RC0 + b * ROUNDS + i)
                for j in range(2):
                    ex = i * 4 + j * 2
                    mm = pe.matmul(pC[:, j * T:(j + 1) * T],
                                   sel_expert[:, bass.ds(ex % HALF, 2), :].rearrange("p a m -> p (a m)"),
                                   rw_split[:, bass.ds(ex // HALF, 1), :].rearrange("p a t -> p (a t)"),
                                   start=True, stop=True)
                mm.then_inc(s["rw_filled"], 1)

            def gate_up(b, i, j):
                k = b * PAIRS + i * 2 + j
                pe.wait_ge(s[f"gu_loaded{j}"], b * (ROUNDS * 16) + i * 16 + 16)
                pe.wait_ge(s["hm2_done"], HM20 + k)
                for g in range(2):
                    for c in range(2):
                        mm = pe.matmul(pG[:, g * 256:g * 256 + T], gu_w[:, j, c, g, :], h1T[:, c, :],
                                       start=(c == 0), stop=(c == 1))
                mm.then_inc(s["gu_done"], 1)

            def down(b, i, j):
                k = b * PAIRS + i * 2 + j
                pe.wait_ge(s[f"dn_loaded{j}"], b * (ROUNDS * 16) + i * 16 + 16)
                pe.wait_ge(s["hm_ready"], HM0 + 1 + k)
                for t in range(2):
                    mm = pe.matmul(pM[0:TT, t * E:(t + 1) * E], hm[:, j, t * TT:(t + 1) * TT], dn_w[:, j, :],
                                   start=False, stop=False, skip_group_check=True)
                mm.then_inc(s["dn_done"], 1)

            def moe(b):
                zero_moe(b)
                with pe.Fori(0, ROUNDS) as i:
                    expert_weights(b, i)
                    gate_up(b, i, 0)
                    gate_up(b, i, 1)
                    down(b, i, 0)
                    down(b, i, 1)

            pe.wait_ge(s["w_in"], W_ALL)
            pe.wait_ge(s["ones_set"], 1)
            pe.wait_ge(s["zeros_set"], 1)
            pe.wait_ge(s["sel_ready"], 1)

            def image(b):
                front(b)
                scan(b)
                tail(b)
                moe(b)

            image(0)
            with pe.Fori(1, NB) as b:
                image(b)

        @block.scalar
        def _(act):
            def norm_root(kind, b):
                act.wait_ge(s["var_" + kind], b + 1)
                act.activation(root[:, :], var[:, :], ACT.Sqrt).then_inc(s["root_" + kind], 1)

            def front(b):
                norm_root("front", b)
                act.wait_ge(s["hnT_done"], b + 1)
                for k in range(2):
                    act.activation(hnT[:, k, :], pD[0:EK, 1, k * T:(k + 1) * T], ACT.Identity,
                                   bias=lnb[:, k:k + 1], scale=lnw[:, k:k + 1]).then_inc(s["hnT_ready"], 1)
                act.wait_ge(s["in_done"], b * 3 + 1)
                for c in range(2):
                    act.activation(xpad[:, c, CONV - 1:], pB[:, c * T:(c + 1) * T], ACT.Copy).then_inc(s["xc_copied"], 1)
                act.wait_ge(s["in_done"], b * 3 + 2)
                act.activation(xpad[:, 2, CONV - 1:], pC[:, 0:T], ACT.Copy).then_inc(s["xc_copied"], 1)
                act.activation(zth[:, 0, :], pC[:, T:2 * T], ACT.Tanh, scale=0.5).then_inc(s["z_tanh"], 1)
                act.wait_ge(s["in_done"], b * 3 + 3)
                act.activation(zth[:, 1:3, :], pair(pD[:, 0, :]), ACT.Tanh, scale=0.5).then_inc(s["z_tanh"], 1)
                act.wait_ge(s["conv_ready"], b * 3 + 3)
                act.activation(cth[:, :, :], cacc[:, :, :], ACT.Tanh, scale=0.5).then_inc(s["conv_tanh"], 1)
                act.wait_ge(s["xp_done"], b * 3 + 1)
                act.activation(dtr[:, :], pD[0:R, 1, 0:T], ACT.Copy).then_inc(s["dtr_ready"], 1)
                act.wait_ge(s["dtp_done"], b + 1)
                for c in range(NC):
                    act.activation(vabs[:, c, :], pD[:, c // 2, (c % 2) * T:(c % 2) * T + T], ACT.Abs,
                                   bias=dtb[:, c:c + 1]).then_inc(s["vabs_ready"], 1)
                act.wait_ge(s["vabs_ready"], b * 3 + 3)
                act.activation(vexp[:, :, :], vabs[:, :, :], ACT.Exp, scale=-1.0).then_inc(s["vexp_ready"], 1)

            def decay(b, i, j):
                for c in range(NC):
                    v = b * (ROUNDS * SUB) + i * SUB + (j * 3 + c)
                    act.wait_ge(s["scan_done"], 1 + v)
                    for e in range(2):
                        act.activation(da[:, j * 3 + c, e, 1:T], dt[:, c, 1:T], ACT.Exp,
                                       scale=aneg[:, c, bass.ds(i * 4 + j * 2 + e, 1)]).then_inc(s["da_ready"], 1)

            def copy_c(b, i, j):
                k = b * PAIRS + i * 2 + j
                act.wait_ge(s["c_filled"], 1 + k)
                act.wait_ge(s["hc_done"], HC0 - 3 + k * 3)
                act.activation(cbc[:, j, :, :], pair(pC), ACT.Copy).then_inc(s["c_copied"], 1)

            def scan(b):
                act.wait_ge(s["u_ready"], b + 1)
                with act.Fori(0, ROUNDS) as i:
                    for j in range(2):
                        copy_c(b, i, j)
                        decay(b, i, j)

            def tail(b):
                norm_root("tail", b)
                act.wait_ge(s["h1T_done"], b + 1)
                act.activation(h1T[:, :, :], pair(pD[0:EK, 1, :]), ACT.Copy).then_inc(s["h1T_ready"], 1)
                act.wait_ge(s["logit_ready"], b + 1)
                act.wait_ge(s["nmax_ready"], b + 1)
                for t in range(2):
                    act.activation(lexp[:, t, :], logit[:, t, :], ACT.Exp,
                                   bias=nmax[:, t:t + 1]).then_inc(s["lexp_ready"], 1)

            def moe_round(b, i):
                act.wait_ge(s["rw_filled"], b * ROUNDS + i + 1)
                act.wait_ge(s["hm_ready"], HM0 + b * PAIRS + i * 2)
                act.activation(rwb[:, :, :], pair(pC), ACT.Copy).then_inc(s["rw_copied"], 1)
                for j in range(2):
                    k = b * PAIRS + i * 2 + j
                    act.wait_ge(s["gu_done"], GU0 + 1 + k)
                    act.activation(gth[:, j, :], pG[:, 0:T], ACT.Tanh, scale=0.5).then_inc(s["g_tanh"], 1)

            def moe(b):
                with act.Fori(0, ROUNDS) as i:
                    moe_round(b, i)

            act.wait_ge(s["w_in"], W_ALL)
            act.activation(alog[:, :, :], alog[:, :, :], ACT.Exp).then_inc(s["a_exp"], 1)
            act.wait_ge(s["a_exp"], 1)
            act.mul(aneg[:, :, :], alog[:, :, :], -1.0).then_inc(s["a_ready"], 1)
            act.wait_ge(s["a_ready"], 1)
            act.wait_ge(s["da_reset"], 1)

            def image(b):
                front(b)
                scan(b)
                tail(b)
                moe(b)
                norm_root("finish", b)

            image(0)
            with act.Fori(1, NB) as b:
                image(b)

        @block.vector
        def _(dve):
            class Steps:

                def __init__(self, name, b, per):
                    self.sem, self.base, self.per, self.n = s[name], b * per, per, 0

                def done(self, ins):
                    ins.then_inc(self.sem, 1)
                    self.n += 1

                def wait(self):
                    dve.wait_ge(self.sem, self.base + self.n)

                def end(self):
                    assert self.n == self.per, (self.n, self.per)

            def settle():
                dve.sem_inc(s["settled"], 1)

            def norm_scale(src, st, kind, b):
                for t in range(2):
                    st.done(dve.bn_stats(stats[:, t, :], src[:, t, :]))
                st.wait()
                settle()
                for t in range(2):
                    st.done(dve.bn_aggr(mv[:, t, :], stats[:, t, :]))
                st.wait()
                dve.tensor_scalar(var[:, :], mv[:, :, 1], EPS, None, ALU.add).then_inc(s["var_" + kind], 1)
                dve.wait_ge(s["var_" + kind], b + 1)
                dve.wait_ge(s["root_" + kind], b + 1)
                st.done(dve.reciprocal(rstd[:, :], root[:, :]))
                st.wait()
                st.done(dve.tensor_tensor(newton[:, :], rstd[:, :], rstd[:, :], ALU.mult))
                st.wait()
                st.done(dve.scalar_tensor_tensor(newton[:, :], newton[:, :], -0.5, var[:, :], ALU.mult, ALU.mult))
                st.wait()
                st.done(dve.scalar_tensor_tensor(rstd[:, :], newton[:, :], 1.5, rstd[:, :], ALU.add, ALU.mult))
                st.wait()

            def layer_norm(src, dst, st, kind, b, ready):
                norm_scale(src, st, kind, b)
                for t in range(2):
                    dve.tensor_scalar(dst[:, t, :], src[:, t, :], mv[:, t, 0:1], rstd[:, t:t + 1],
                                      ALU.subtract, ALU.mult).then_inc(ready, 1)

            def split3(parts, rest, src, st, last):
                st.done(dve.tensor_copy(parts[0:96], src))
                st.wait()
                st.done(dve.tensor_tensor(rest[0:96], src, parts[0:96], ALU.subtract))
                st.wait()
                st.done(dve.tensor_copy(parts[32:64], rest[32:64]))
                st.done(dve.tensor_copy(parts[64:96], rest[64:96]))
                st.wait()
                last(dve.tensor_tensor(parts[64:96], rest[64:96], parts[64:96], ALU.subtract))

            def front(b):
                st = Steps("front_v", b, 43)
                dve.wait_ge(s["embed_done"], b + 1)
                st.done(dve.tensor_copy(h[:, :, :], pair(pD[0:TT, 0, :])))
                st.wait()
                layer_norm(h, hn, st, "front", b, s["hn_ready"])
                dve.wait_ge(s["z_tanh"], b * 2 + 1)
                dve.scalar_tensor_tensor(gate[:, 0, :], zth[:, 0, :], 1.0, pC[:, T:2 * T], ALU.add,
                                         ALU.mult).then_inc(s["gate_ready"], 1)
                dve.wait_ge(s["z_tanh"], b * 2 + 2)
                for c in (1, 2):
                    dve.scalar_tensor_tensor(gate[:, c, :], zth[:, c, :], 1.0, pD[:, 0, (c - 1) * T:c * T], ALU.add,
                                             ALU.mult).then_inc(s["gate_ready"], 1)
                dve.wait_ge(s["xc_copied"], b * 3 + 3)
                for k in range(CONV):
                    for c in range(NC):
                        tap, w = xpad[:, c, k:k + T], convw[:, c, k:k + 1]
                        if k == 0:
                            ins = dve.tensor_scalar(cacc[:, c, :], tap, w, convb[:, c:c + 1], ALU.mult, ALU.add)
                        else:
                            ins = dve.scalar_tensor_tensor(cacc[:, c, :], tap, w, cacc[:, c, :], ALU.mult, ALU.add)
                        if k == CONV - 1:
                            ins.then_inc(s["conv_ready"], 1)
                        else:
                            st.done(ins)
                    if k < CONV - 1:
                        st.wait()
                dve.wait_ge(s["conv_tanh"], b + 1)
                st.done(dve.tensor_scalar(cth[:, :, :], cth[:, :, :], 0.5, 0.5, ALU.mult, ALU.add))
                st.wait()
                dve.tensor_tensor(xs[:, :, :], cth[:, :, :], cacc[:, :, :], ALU.mult).then_inc(s["xs_ready"], 1)
                for q, p in ((0, pB), (1, pC)):
                    dve.wait_ge(s["xp_done"], b * 3 + 2 + q)
                    split3(bc_split[:, q], bc_rest[:, q], pair(p[0:96, :]), st,
                           lambda ins: ins.then_inc(s["bc_ready"], 1))
                dve.wait_ge(s["vabs_ready"], b * 3 + 3)
                for c in range(NC):
                    st.done(dve.tensor_scalar(vmax[:, c, :], pD[:, c // 2, (c % 2) * T:(c % 2) * T + T],
                                              dtb[:, c:c + 1], 0.0, ALU.add, ALU.max))
                dve.wait_ge(s["vexp_ready"], b + 1)
                q = LOG1P_Q
                st.done(dve.tensor_scalar(poly[:, :, :], vexp[:, :, :], q[-1], None, ALU.mult))
                for k in range(len(q) - 2, -1, -1):
                    st.wait()
                    st.done(dve.scalar_tensor_tensor(poly[:, :, :], poly[:, :, :], q[k], vexp[:, :, :], ALU.add, ALU.mult))
                st.wait()
                st.done(dve.tensor_tensor(dt[:, :, :], poly[:, :, :], vmax[:, :, :], ALU.add))
                st.wait()
                dve.tensor_tensor(u[:, :, :], dt[:, :, :], xs[:, :, :], ALU.mult).then_inc(s["u_ready"], 1)
                st.end()

            def products(b, i, j, c):
                m = j * 3 + c
                v = b * (ROUNDS * SUB) + i * SUB + m
                if c == 0:
                    dve.wait_ge(s["b_filled"], 1 + b * PAIRS + i * 2 + j)
                dve.wait_ge(s["scan_done"], SCAN0 - 1 + v)
                dve.tensor_tensor(pair(pD[:, m % 2, :]), u[:, c:c + 1, :].to_broadcast([128, 2, T]), pair(pB),
                                  ALU.mult).then_inc(s["dbx_done"], 1)

            def recur(b, i, j, c):
                m = j * 3 + c
                v = b * (ROUNDS * SUB) + i * SUB + m
                dve.wait_ge(s["dbx_done"], DBX0 + 1 + v)
                dve.wait_ge(s["da_ready"], 2 + v * 2)
                dve.wait_ge(s["hc_done"], 1 + v)
                dve.tensor_tensor_scan(hs[:, m].rearrange("p a t -> p (a t)"), da[:, m].rearrange("p a t -> p (a t)"),
                                       pD[:, m % 2, 0:2 * T], 0.0, ALU.mult, ALU.add).then_inc(s["scan_done"], 1)

            def scan_round(b, i):
                units = [(j, c) for j in range(2) for c in range(NC)]
                for m, (j, c) in enumerate(units):
                    products(b, i, j, c)
                    if m >= 1:
                        recur(b, i, *units[m - 1])
                recur(b, i, *units[-1])

            def scan(b):
                dve.wait_ge(s["u_ready"], b + 1)
                settle()
                with dve.Fori(0, ROUNDS) as i:
                    scan_round(b, i)

            def tail(b):
                dve.wait_ge(s["y_added"], YA0 + (b + 1) * (ROUNDS * SUB))
                for c in range(NC):
                    dve.scalar_tensor_tensor(yt[:, c, :], xs[:, c, :], dsk[:, c:c + 1], y_of(c), ALU.mult,
                                             ALU.add).then_inc(s["y_taken"], 1)
                dve.wait_ge(s["y_taken"], b * 3 + 3)
                dve.scalar_tensor_tensor(yg[:, :, :], yt[:, :, :], 0.5, gate[:, :, :], ALU.mult,
                                         ALU.mult).then_inc(s["yg_ready"], 1)
                st = Steps("tail_v", b, 22)
                dve.wait_ge(s["op_done"], b + 1)
                st.done(dve.scalar_tensor_tensor(res[:, :, :], h[:, :, :], 2.0, pair(pD[0:TT, 0, :]), ALU.mult, ALU.add))
                st.wait()
                norm_scale(res, st, "tail", b)
                st.done(dve.tensor_scalar(h1[:, 0, :], res[:, 0, :], mv[:, 0, 0:1], rstd[:, 0:1], ALU.subtract, ALU.mult))
                st.wait()
                dve.tensor_scalar(h1[:, 1, :], res[:, 1, :], mv[:, 1, 0:1], rstd[:, 1:2], ALU.subtract,
                                  ALU.mult).then_inc(s["h1_ready"], 1)
                dve.wait_ge(s["rt_done"], b + 1)
                dve.tensor_copy(logit[:, :, :], pB[0:TT, 0:128].rearrange("p (t e) -> p t e", t=2)).then_inc(s["logit_ready"], 1)
                dve.wait_ge(s["logit_ready"], b + 1)
                settle()
                for t in range(2):
                    st.done(dve.max(top8[:, t, :], logit[:, t, :]))
                st.wait()
                dve.tensor_scalar(nmax[:, :], top8[:, :, 0], -1.0, None, ALU.mult).then_inc(s["nmax_ready"], 1)
                for t in range(2):
                    st.done(dve.match_replace(lrest[:, t, :], top8[:, t, :], logit[:, t, :], -3.0e38))
                st.wait()
                st.done(dve.tensor_tensor(lmask[:, :, :], lrest[:, :, :], logit[:, :, :], ALU.not_equal))
                st.wait()
                dve.wait_ge(s["lexp_ready"], b * 2 + 2)
                for t in range(2):
                    st.done(dve.scalar_tensor_tensor(lmask[:, t, :], lmask[:, t, :], 1.0, lexp[:, t, :], ALU.mult, ALU.mult,
                                                     accum_out=wsum[:, t:t + 1]))
                st.wait()
                st.done(dve.reciprocal(winv[:, :], wsum[:, :]))
                st.wait()
                for t in range(2):
                    dve.tensor_scalar(wrep[:, t].rearrange("p a s e -> p a s e"),
                                      lmask[:, t, :].rearrange("p (a o e) -> p a o e", a=2, o=1).to_broadcast([TT, 2, 3, HALF]),
                                      winv[:, t:t + 1], 0.5, ALU.mult, ALU.mult).then_inc(s["wrep_ready"], 1)
                dve.wait_ge(s["wT_done"], b + 1)
                split3(rw_split, rw_rest, pair(pC[0:96, :]), st, lambda ins: ins.then_inc(s["rw_ready"], 1))
                st.end()

            def moe_pair(b, i, j):
                k = b * PAIRS + i * 2 + j
                dve.wait_ge(s["g_tanh"], 1 + k)
                dve.wait_ge(s["hm2_done"], HM20 + k)
                dve.scalar_tensor_tensor(hm1[:, j, :], gth[:, j, :], 1.0, pG[:, 0:T], ALU.add,
                                         ALU.mult).then_inc(s["hm1_done"], 1)
                dve.wait_ge(s["hm1_done"], 1 + k)
                dve.wait_ge(s["hm_ready"], HM0 - 1 + k)
                dve.tensor_tensor(hm2[:, j, :], hm1[:, j, :], pG[:, 256:256 + T], ALU.mult).then_inc(s["hm2_done"], 1)

            def moe(b):
                with dve.Fori(0, ROUNDS) as i:
                    for j in range(2):
                        moe_pair(b, i, j)

            def finish(b):
                st = Steps("finish_v", b, 9)
                dve.wait_ge(s["dn_done"], DN0 + (b + 1) * PAIRS)
                if not isinstance(b, int):
                    dve.wait_ge(s["stored"], b * 16)
                st.done(dve.tensor_tensor(ores[:, :, :], h1[:, :, :], pair(pM[0:TT, :]), ALU.add))
                st.wait()
                layer_norm(ores, outb, st, "finish", b, s["out_ready"])
                st.end()

            dve.memset(zero_w[:, :], 0.0)
            dve.memset(zero_x[:, :], 0.0).then_inc(s["zeros_set"], 1)
            dve.memset(ones[:, :], 1.0).then_inc(s["ones_set"], 1)
            dve.memset(xpad[:, :, 0:CONV - 1], 0.0).then_inc(s["pad_set"], 1)
            dve.memset(da[:, :, :, 0:1], 0.0).then_inc(s["da_reset"], 1)
            dve.wait_ge(s["pad_set"], 1)
            dve.wait_ge(s["w_in"], W_ALL)
            dve.tensor_copy(sel_state[:, :, :], eye[:, :].rearrange("p (a o) -> p a o", o=1).to_broadcast([96, HALF, 128]))
            dve.tensor_copy(sel_expert[:, :, :], eye[:, :].rearrange("p (a o) -> p a o", o=1).to_broadcast([96, HALF, 64])
                            ).then_inc(s["sel_ready"], 1)

            def image(b):
                front(b)
                scan(b)
                tail(b)
                moe(b)
                finish(b)

            image(0)
            with dve.Fori(1, NB) as b:
                image(b)

        @block.gpsimd
        def _(pool):
            for name, n in (("dbx_done", DBX0), ("scan_done", SCAN0), ("hc_done", HC0), ("y_added", YA0),
                            ("c_copied", CC0), ("rw_copied", RC0), ("gu_done", GU0), ("dn_done", DN0),
                            ("hm2_done", HM20), ("hm_ready", HM0)):
                pool.sem_inc(s[name], n)

            def scan(b):
                with pool.Fori(0, ROUNDS) as i:
                    for j in range(2):
                        k = b * PAIRS + i * 2 + j
                        pool.wait_ge(s["c_copied"], CC0 + 1 + k)
                        for c in range(NC):
                            m = j * 3 + c
                            v = b * (ROUNDS * SUB) + i * SUB + m
                            pool.wait_ge(s["scan_done"], SCAN0 + 1 + v)
                            pool.wait_ge(s["y_added"], 1 + v)
                            pool.tensor_tensor(hc[:, m], hs[:, m], cbc[:, j], ALU.mult).then_inc(s["hc_done"], 1)

            def moe(b):
                with pool.Fori(0, ROUNDS) as i:
                    for j in range(2):
                        k = b * PAIRS + i * 2 + j
                        pool.wait_ge(s["hm2_done"], HM20 + 1 + k)
                        pool.wait_ge(s["rw_copied"], RC0 + b * ROUNDS + i + 1)
                        pool.wait_ge(s["dn_done"], 1 + k)
                        pool.tensor_tensor(hm[:, j, :], hm2[:, j, :], rwb[:, j, :], ALU.mult).then_inc(s["hm_ready"], 1)

            scan(0)
            moe(0)
            with pool.Fori(1, NB) as b:
                scan(b)
                moe(b)


LOG1P_Q = log1p_coefficients()


def kernel(**inputs):
    import numpy as np
    import concourse.bacc as bacc
    from concourse import mybir as mb
    from concourse.bass_utils import run_bass_kernel_spmd as run

    a = {k: np.asarray(v) for k, v in inputs.items()}
    p = "L0_attn_"

    def chunks(w, n):
        return w.reshape(n, w.shape[0] // n, *w.shape[1:]).swapaxes(0, 1)

    xp = a[p + "x_proj_w"]
    rows = [xp[:R]] + [xp[R + q * HALF:R + (q + 1) * HALF] for q in range(4) for _ in range(3)]
    gate, up = a["L0_ffn_w_gate"], a["L0_ffn_w_up"]
    gu = np.stack([gate, up]).reshape(2, PAIRS, 2, 2, EK, 64)
    arrays = {
        "x": a["x"].reshape(NB, 3, 8, 16, 8, 16).transpose(0, 3, 5, 1, 2, 4).reshape(NB, 2, 128, T).transpose(0, 2, 1, 3),
        "tok_w": chunks(a["L0_tok_W"], 2),
        "tok_b": a["L0_tok_b"].reshape(1, E),
        "ln_w": a[p + "ln_w"].reshape(2, EK).T,
        "ln_b": a[p + "ln_b"].reshape(2, EK).T,
        "in_w": chunks(a[p + "in_proj_w"].T, 2),
        "conv_w": chunks(a[p + "conv_w"].reshape(NC * 128, CONV), NC),
        "conv_b": a[p + "conv_b"].reshape(NC, 128).T,
        "xp_w": chunks(np.concatenate(rows).T, NC),
        "dtp_w": a[p + "dt_proj_w"].T,
        "dtp_b": a[p + "dt_proj_b"].reshape(NC, 128).T,
        "a_log": chunks(a[p + "A_log"], NC),
        "d_skip": a[p + "D"].reshape(NC, 128).T,
        "out_w": chunks(a[p + "out_proj_w"].T, NC),
        "router_w": chunks(a["L0_ffn_router_w"].T, 2),
        "wgu": gu.transpose(4, 1, 3, 0, 2, 5).reshape(EK, PAIRS, 512),
        "wd": a["L0_ffn_w_down"].reshape(PAIRS, 128, E).transpose(1, 0, 2),
        "ident": np.eye(128, dtype=np.float32),
        "eye3": np.tile(np.eye(HALF, dtype=np.float32), (3, 1)),
    }
    arrays = {k: np.ascontiguousarray(v) for k, v in arrays.items()}
    nc = bacc.Bacc("TRN2", target_bir_lowering=False, num_devices=1)
    aps = {k: nc.dram_tensor(k, v.shape, mb.dt.from_np(v.dtype), kind="ExternalInput").ap() for k, v in arrays.items()}
    out = nc.dram_tensor("out", (NB, T, E), F32, kind="ExternalOutput").ap()
    vit_mamba_moe(nc, out=out, **aps)
    r = run(nc, [arrays], core_ids=[0])
    return r.results[0]["out"]
```

```python
from contextlib import ExitStack

import concourse.bass as bass
from concourse import mybir

F32 = mybir.dt.float32
BF16 = mybir.dt.bfloat16
I32 = mybir.dt.int32
ALU = mybir.AluOpType
ACT = mybir.ActivationFunctionType

NB = 4
T = 192
TT = 96
E = 192
EK = 96
NC = 3
N = 64
R = 12
CONV = 4
PAIRS = 32
HALF = 32
ROUNDS = 16
PER_ROUND = 1
NEWTON = 3
RSQRT_MAGIC = float(0x5f3759df)
DEG = 8
SUB = 6
RING = 2 * SUB
EPS = 1e-5



def log1p_coefficients():
    import numpy as np
    at = 0.5 + 0.5 * np.cos(np.pi * (np.arange(DEG + 1) + 0.5) / (DEG + 1))
    cheb = np.polynomial.Chebyshev.fit(at, np.log1p(at) / at, DEG, domain=[0, 1])
    return [float(c) for c in cheb.convert(kind=np.polynomial.Polynomial).coef]


def gap_steps():
    chain = ["F1", "T1", "F2", "T2", "F3", "T4", "F4", "T5", "F5", "T6", "F6", "T7", "F7", "T8", "F8"]
    steps, k = [], ROUNDS * PER_ROUND
    for name in chain:
        steps.append((name, 0))
        if k < PAIRS:
            steps.append(("G", k))
            if k > ROUNDS * PER_ROUND:
                steps.insert(len(steps) - 2, ("H", k - 1))
                steps.append(("D", k - 1))
            k += 1
    for last in range(k, PAIRS + 1):
        if k > ROUNDS * PER_ROUND:
            steps.append(("H", last - 1))
            steps.append(("D", last - 1))
        if last < PAIRS:
            steps.append(("G", last))
    return steps + [("finish", 0), ("commit", 0)]


def vit_mamba_moe(nc, x, tok_w, tok_b, ln_w, ln_b, in_w, conv_w, conv_b, xp_w, dtp_w, dtp_b, a_log, d_skip, out_w,
                  router_w, wgu, wd, ident, eye3, out):
    with ExitStack() as ctx:
        def sb(name, shape, dt=F32):
            return ctx.enter_context(nc.sbuf_tensor(name, shape, dt))

        def bank(name, dt=F32):
            return ctx.enter_context(nc.psum_tensor(name, [128, 512], dt))

        def sem(name):
            return ctx.enter_context(nc.semaphore(name))

        tokw = sb("tokw", [128, 2, E])
        tokb = sb("tokb", [1, E])
        ones = sb("ones", [1, TT])
        lnw = sb("lnw", [EK, 2])
        lnb = sb("lnb", [EK, 2])
        inw = sb("inw", [EK, 2, 2 * NC * 128])
        convw = sb("convw", [128, NC, CONV])
        convb = sb("convb", [128, NC])
        xpw = sb("xpw", [128, NC, R + 4 * 96])
        dtw = sb("dtw", [R, NC * 128])
        dtb = sb("dtb", [128, NC])
        alog = sb("alog", [128, NC, N])
        aneg = sb("aneg", [128, NC, N])
        dsk = sb("dsk", [128, NC])
        outw = sb("outw", [128, NC, E])
        rw_w = sb("rw_w", [EK, 2, 64])
        idn = sb("idn", [128, 128])
        eye = sb("eye", [96, HALF])
        sel_state = sb("sel_state", [96, HALF, 128], BF16)
        sel_expert = sb("sel_expert", [96, HALF, 64], BF16)
        zero_w = sb("zero_w", [1, 128], BF16)
        zero_x = sb("zero_x", [1, 2 * T], BF16)

        xb = sb("xb", [128, 2, T])
        h = sb("h", [TT, 2, E])
        norms = ("front", "tail", "finish")
        stats, mv, var, newton, rstd = ({q: sb(n + q, [TT, 2] + f) for q in norms} for n, f in (
            ("stats_", [6]), ("mv_", [2]), ("var_", []), ("newton_", []), ("rstd_", [])))
        hn = sb("hn", [TT, 2, E])
        hnT = sb("hnT", [EK, 2, T])
        xpad = sb("xpad", [128, NC, CONV - 1 + T])
        zth = sb("zth", [128, NC, T])
        gate = sb("gate", [128, NC, T])
        cacc = sb("cacc", [128, NC, T])
        cth = sb("cth", [128, NC, T])
        xs = sb("xs", [128, NC, T])
        dtr = sb("dtr", [R, T])
        vabs = sb("vabs", [128, NC, T])
        vexp = sb("vexp", [128, NC, T])
        vmax = sb("vmax", [128, NC, T])
        poly = sb("poly", [128, NC, T])
        dt = sb("dt", [128, NC, T])
        u = sb("u", [128, NC, T])
        bc_split = sb("bc_split", [96, 2, 2, T], BF16)
        bc_rest = sb("bc_rest", [96, 2, 2, T])
        yt = sb("yt", [128, NC, T])
        yg = sb("yg", [128, NC, T])
        res = sb("res", [TT, 2, E])
        h1n = sb("h1n", [TT, 2, E])
        h1Tn = sb("h1Tn", [EK, 2, T])
        h1 = sb("h1", [TT, 2, E])
        h1T = sb("h1T", [EK, 2, T])
        logit = sb("logit", [TT, 2, 64])
        top8 = sb("top8", [TT, 2, 8])
        nmax = sb("nmax", [TT, 2])
        lrest = sb("lrest", [TT, 2, 64])
        lexp = sb("lexp", [TT, 2, 64])
        lmask = sb("lmask", [TT, 2, 64])
        wsum = sb("wsum", [TT, 2])
        winv = sb("winv", [TT, 2])
        wrep = sb("wrep", [TT, 2, 2, 3, HALF])
        rw_new = sb("rw_new", [96, 2, T], BF16)
        rw_split = sb("rw_split", [96, 2, T], BF16)
        rw_rest = sb("rw_rest", [96, 2, T])
        ores = sb("ores", [TT, 2, E])
        outb = sb("outb", [TT, 2, E])

        da = sb("da", [128, RING, 2, T])
        hs = sb("hs", [128, RING, 2, T])
        hc = sb("hc", [128, RING, 2, T])
        cbc = sb("cbc", [128, 4, 2, T])
        gu_w = sb("gu_w", [EK, 2, 2, 2, 128])
        dn_w = sb("dn_w", [128, 2, E])
        rwb = sb("rwb", [128, PAIRS, T])
        gth = sb("gth", [128, 2, T])
        hm1 = sb("hm1", [128, 2, T])
        hm2 = sb("hm2", [128, 2, T])
        hm = sb("hm", [128, 2, T])

        pD = ctx.enter_context(nc.psum_tensor("pD", [128, 2, 512], F32))
        pBC = [bank("pBC0"), bank("pBC1")]
        pY = ctx.enter_context(nc.psum_tensor("pY", [128, 2, 512], F32))
        pG = bank("pG")
        pM = bank("pM")

        def y_of(c):
            return pY[:, c // 2, (c % 2) * T:(c % 2) * T + T]

        def pair(ap, w=T):
            return ap[:, 0:2 * w].rearrange("p (a t) -> p a t", a=2)

        names = """w_in x_in zeros_set ones_set pad_set da_reset a_exp a_ready sel_ready embed_done hn_ready hnT_done
            hnT_ready in_done xc_copied z_tanh gate_ready conv_ready conv_tanh xs_ready xp_done dtr_ready bc_ready dtp_done
            vabs_ready vexp_ready u_ready b_filled c_filled c_copied dbx_done da_ready scan_done
            hc_done y_added y_taken yg_ready op_done h1n_ready h1T_done h1T_ready rt_done logit_ready nmax_ready lexp_ready
            wrep_ready wT_done rwn_ready committed gu_loaded0 gu_loaded1 dn_loaded0 dn_loaded1 gu_done dn_done rw_filled
            rw_copied g_tanh hm1_done hm2_done hm_ready out_ready stored settled
            front_v tail_v finish_v""".split()
        s = {n: sem(n) for n in names}

        WEIGHTS = [(tokw, tok_w), (tokb, tok_b), (idn, ident), (eye, eye3), (lnw, ln_w), (lnb, ln_b), (inw, in_w),
                   (convw, conv_w), (convb, conv_b), (xpw, xp_w), (dtw, dtp_w), (dtb, dtp_b), (alog, a_log),
                   (dsk, d_skip), (outw, out_w), (rw_w, router_w)]
        W_ALL = 16 * len(WEIGHTS)
        out_v = out.rearrange("b (t p) e -> p (b t) e", t=2)

        DBX0, SCAN0, HC0, YA0, CC0, RC0, GU0, DN0, HM20, HM0 = 3, RING, RING, RING, 1, 1, 2, 2, 1, 2

        block = ctx.enter_context(nc.Block())
        gap = gap_steps()

        def walk(parts, b, tail=True, front=True, moe=True):
            for name, k in gap:
                if name in ("G", "H", "D"):
                    if moe and name in parts:
                        parts[name](b - 1, k)
                elif name == "finish":
                    if moe and name in parts:
                        parts[name](b - 1)
                elif name[0] == "F":
                    if front and name in parts:
                        parts[name](b + 1)
                elif tail and name in parts:
                    parts[name](b)

        def images(front0, scan, parts, moe_alone):
            front0()
            scan(0, False)
            walk(parts, 0, moe=False)
            with images.engine.Fori(1, NB - 1) as b:
                scan(b, True)
                walk(parts, b)
            scan(NB - 1, True)
            walk(parts, NB - 1, front=False)
            moe_alone(NB - 1)

        def front_only(parts):
            for name, _ in gap:
                if name[0] == "F" and name in parts:
                    parts[name](0)

        @block.sync
        def _(sp):
            sp.dma_start(xb[:, :, :], x[0]).then_inc(s["x_in"], 16)
            for dst, src in WEIGHTS:
                sp.dma_start(dst[tuple(slice(None) for _ in dst.shape)], src).then_inc(s["w_in"], 16)

            def load_x(b):
                sp.wait_ge(s["embed_done"], b)
                sp.dma_start(xb[:, :, :].rearrange("p k t -> p (k t)"),
                             x.rearrange("b p k t -> p b (k t)")[:, bass.ds(b, 1), :]).then_inc(s["x_in"], 16)

            def load_experts(b):
                with sp.Fori(0, ROUNDS) as i:
                    for j in range(2):
                        sp.wait_ge(s["gu_done"], b * PAIRS + i * 2 + (j + 1))
                        sp.dma_start(gu_w[:, j].rearrange("p k g c -> p (k g c)"),
                                     wgu[:, bass.ds(i * 2 + j, 1), :]).then_inc(s[f"gu_loaded{j}"], 16)
                        sp.wait_ge(s["dn_done"], b * PAIRS + i * 2 + (j + 1))
                        sp.dma_start(dn_w[:, j, :], wd[:, bass.ds(i * 2 + j, 1), :]).then_inc(s[f"dn_loaded{j}"], 16)

            def store(b):
                sp.wait_ge(s["out_ready"], b * 2 + 2)
                sp.dma_start(out_v[:, bass.ds(b * 2, 2), :], outb[:, :, :]).then_inc(s["stored"], 16)

            load_x(1)
            with sp.Fori(0, NB - 2) as b:
                load_x(b + 2)
                load_experts(b)
                store(b)
            load_experts(NB - 2)
            store(NB - 2)
            load_experts(NB - 1)
            store(NB - 1)
            sp.wait_ge(s["stored"], 16 * NB)

        @block.tensor
        def _(pe):
            def embed(b):
                pe.wait_ge(s["x_in"], b * 16 + 16)
                for t in range(2):
                    o = pD[0:TT, 0, t * E:(t + 1) * E]
                    for k in range(2):
                        pe.matmul(o, xb[:, k, t * TT:(t + 1) * TT], tokw[:, k, :], start=(k == 0), stop=False)
                    mm = pe.matmul(o, ones[0:1, :], tokb[0:1, :], start=False, stop=True)
                mm.then_inc(s["embed_done"], 1)

            def hn_transposed(b):
                pe.wait_ge(s["hn_ready"], b * 2 + 2)
                for k in range(2):
                    for t in range(2):
                        mm = pe.transpose(pD[0:EK, 1, k * T + t * TT:k * T + (t + 1) * TT],
                                          hn[:, t, k * EK:(k + 1) * EK], idn[0:TT, 0:TT])
                mm.then_inc(s["hnT_done"], 1)

            def in_proj(b):
                pe.wait_ge(s["hnT_ready"], b * 2 + 2)
                for m in range(6):
                    o = [pBC[0], pD[:, 0, :], pD[:, 1, :]][m // 2][:, (m % 2) * T:(m % 2) * T + T]
                    for k in range(2):
                        mm = pe.matmul(o, inw[:, k, m * 128:(m + 1) * 128], hnT[:, k, :], start=(k == 0), stop=(k == 1))
                    if m % 2:
                        mm.then_inc(s["in_done"], 1)

            def x_proj(b):
                pe.wait_ge(s["xs_ready"], b + 1)
                pe.wait_ge(s["xc_copied"], b * 3 + 3)
                pe.wait_ge(s["gate_ready"], b * 3 + 3)
                for c in range(NC):
                    mm = pe.matmul(pD[0:R, 1, 0:T], xpw[:, c, 0:R], xs[:, c, :], start=(c == 0), stop=(c == 2))
                mm.then_inc(s["xp_done"], 1)
                for q in range(4):
                    o = [pBC[0], pD[:, 0, :]][q // 2][0:96, (q % 2) * T:(q % 2) * T + T]
                    for c in range(NC):
                        mm = pe.matmul(o, xpw[:, c, R + q * 96:R + (q + 1) * 96], xs[:, c, :],
                                       start=(c == 0), stop=(c == 2))
                    if q % 2:
                        mm.then_inc(s["xp_done"], 1)

            def dt_proj(b):
                pe.wait_ge(s["dtr_ready"], b + 1)
                pe.wait_ge(s["bc_ready"], b * 2 + 2)
                for c in range(NC):
                    o = pD[:, c // 2, (c % 2) * T:(c % 2) * T + T]
                    mm = pe.matmul(o, dtw[:, c * 128:(c + 1) * 128], dtr[:, :], start=True, stop=True)
                mm.then_inc(s["dtp_done"], 1)

            def fill_b(b, i, j):
                k = b * PAIRS + i * 2 + j
                pe.wait_ge(s["c_copied"], CC0 + k)
                spread(0, i, j, pBC[j]).then_inc(s["b_filled"], 1)

            def fill_c(b, i, j):
                pe.wait_ge(s["dbx_done"], DBX0 + (b * PAIRS + i * 2 + j) * 3)
                spread(1, i, j, pBC[1 - j]).then_inc(s["c_filled"], 1)

            def spread(which, i, j, bank_):
                for e in range(2):
                    n = i * 4 + j * 2 + e
                    mm = pe.matmul(bank_[:, e * T:(e + 1) * T],
                                   sel_state[:, bass.ds(n % HALF, 1), :].rearrange("p a m -> p (a m)"),
                                   bc_split[:, which, bass.ds(n // HALF, 1), :].rearrange("p a t -> p (a t)"),
                                   start=True, stop=True)
                return mm

            def add_y(b, i, j, r):
                for c in range(NC):
                    v = b * (ROUNDS * SUB) + i * SUB + (j * 3 + c)
                    pe.wait_ge(s["hc_done"], HC0 + 1 + v)
                    for e in range(2):
                        mm = pe.matmul(y_of(c), idn[:, :], hc[:, r * SUB + j * 3 + c, e, :], start=False, stop=False,
                                       skip_group_check=True)
                    mm.then_inc(s["y_added"], 1)

            def expert_weights(b, i):
                for j in range(2):
                    ex = i * 4 + j * 2
                    mm = pe.matmul(pBC[1][:, j * T:(j + 1) * T],
                                   sel_expert[:, bass.ds(ex % HALF, 2), :].rearrange("p a m -> p (a m)"),
                                   rw_split[:, bass.ds(ex // HALF, 1), :].rearrange("p a t -> p (a t)"),
                                   start=True, stop=True)
                mm.then_inc(s["rw_filled"], 1)

            def gate_up(b, k, half=None):
                slot = k % 2 if half is None else half[1]
                turn = k // 2 if half is None else half[0]
                pe.wait_ge(s[f"gu_loaded{slot}"], b * (ROUNDS * 16) + turn * 16 + 16)
                pe.wait_ge(s["hm2_done"], HM20 + b * PAIRS + k)
                for g in range(2):
                    for c in range(2):
                        mm = pe.matmul(pG[:, g * 256:g * 256 + T], gu_w[:, slot, c, g, :], h1T[:, c, :],
                                       start=(c == 0), stop=(c == 1))
                mm.then_inc(s["gu_done"], 1)

            def down(b, k, half=None):
                slot = k % 2 if half is None else half[1]
                turn = k // 2 if half is None else half[0]
                pe.wait_ge(s[f"dn_loaded{slot}"], b * (ROUNDS * 16) + turn * 16 + 16)
                pe.wait_ge(s["hm_ready"], HM0 + 1 + b * PAIRS + k)
                for t in range(2):
                    mm = pe.matmul(pM[0:TT, t * E:(t + 1) * E], hm[:, slot, t * TT:(t + 1) * TT], dn_w[:, slot, :],
                                   start=False, stop=False, skip_group_check=True)
                mm.then_inc(s["dn_done"], 1)

            def zero_moe(b):
                if not isinstance(b, int) or b > 0:
                    pe.wait_ge(s["out_ready"], b * 2)
                pe.matmul(pM[0:TT, 0:2 * E], zero_w[:, 0:TT], zero_x[:, :], start=True, stop=True)

            def scan(b, moe):
                def turn(i, r):
                    return (i - r) // 2 if isinstance(i, int) else turn.i2

                def experts(kind, i, r, n):
                    if not moe:
                        return
                    k = i * PER_ROUND + n
                    if PER_ROUND == 2:
                        kind(b - 1, k, (i + n // 2, n % 2))
                    else:
                        kind(b - 1, k, (turn(i, r) + (r + n) // 2, (r + n) % 2))

                def first_half(i, r, before):
                    fill_c(b, i, 0)
                    if before:
                        add_y(b, i - 1, 0, 1 - r)
                    if moe:
                        pe.wait_ge(s["c_copied"], CC0 + 1 + b * PAIRS + i * 2)
                        expert_weights(b - 1, i)
                        if before:
                            experts(down, i, r, -1)
                        pe.wait_ge(s["rw_copied"], RC0 + 1 + (b - 1) * ROUNDS + i)
                    fill_b(b, i, 1)
                    if PER_ROUND == 2:
                        experts(gate_up, i, r, 1)

                def second_half(i, r, before, after):
                    fill_c(b, i, 1)
                    if before:
                        add_y(b, i - 1, 1, 1 - r)
                    if after:
                        fill_b(b, i + 1, 0)
                    if PER_ROUND == 2:
                        experts(down, i, r, 0)
                    if after:
                        experts(gate_up, i, r, PER_ROUND)

                if not isinstance(b, int) or b > 0:
                    pe.wait_ge(s["rwn_ready"], b)
                    pe.wait_ge(s["h1T_ready"], b)
                    pe.wait_ge(s["logit_ready"], b)
                for k in range(2):
                    pe.matmul(pY[:, k, 0:2 * T], zero_w[:, :], zero_x[:, :], start=True, stop=True)
                pe.wait_ge(s["bc_ready"], b * 2 + 2)
                fill_b(b, 0, 0)
                if moe:
                    zero_moe(b - 1)
                    pe.wait_ge(s["committed"], b * 3)
                    gate_up(b - 1, 0, (0, 0))
                first_half(0, 0, False)
                second_half(0, 0, False, True)
                with pe.Fori(0, ROUNDS // 2 - 1) as i2:
                    for r in (1, 0):
                        turn.i2 = i2 + (1 - r)
                        i = i2 * 2 + (2 - r)
                        first_half(i, r, True)
                        second_half(i, r, True, True)
                first_half(ROUNDS - 1, 1, True)
                second_half(ROUNDS - 1, 1, True, False)
                for j in range(2):
                    add_y(b, ROUNDS - 1, j, 1)
                experts(down, ROUNDS - 1, 1, PER_ROUND - 1)

            def out_proj(b):
                pe.wait_ge(s["yg_ready"], b + 1)
                if not isinstance(b, int) or b > 0:
                    pe.wait_ge(s["rw_copied"], RC0 + b * ROUNDS)
                for t in range(2):
                    for c in range(NC):
                        mm = pe.matmul(pBC[1][0:TT, t * E:(t + 1) * E], yg[:, c, t * TT:(t + 1) * TT], outw[:, c, :],
                                       start=(c == 0), stop=(c == 2))
                mm.then_inc(s["op_done"], 1)

            def h1_transposed(b):
                pe.wait_ge(s["h1n_ready"], b * 2 + 2)
                for k in range(2):
                    for t in range(2):
                        mm = pe.transpose(pY[0:EK, 0, k * T + t * TT:k * T + (t + 1) * TT],
                                          h1n[:, t, k * EK:(k + 1) * EK], idn[0:TT, 0:TT])
                mm.then_inc(s["h1T_done"], 1)

            def router(b):
                pe.wait_ge(s["h1T_ready"], b + 1)
                for t in range(2):
                    for k in range(2):
                        mm = pe.matmul(pY[0:TT, 1, t * 64:(t + 1) * 64], h1Tn[:, k, t * TT:(t + 1) * TT], rw_w[:, k, :],
                                       start=(k == 0), stop=(k == 1))
                mm.then_inc(s["rt_done"], 1)

            def weights_transposed(b):
                pe.wait_ge(s["wrep_ready"], b * 2 + 2)
                for hf in range(2):
                    for t in range(2):
                        mm = pe.transpose(pBC[1][0:96, hf * T + t * TT:hf * T + (t + 1) * TT],
                                          wrep[:, t, hf].rearrange("p s e -> p (s e)"), idn[0:TT, 0:TT])
                mm.then_inc(s["wT_done"], 1)

            def moe_alone(b):
                zero_moe(b)
                pe.wait_ge(s["committed"], (b + 1) * 3)
                pe.wait_ge(s["rwn_ready"], b + 1)
                with pe.Fori(0, ROUNDS) as i:
                    pe.wait_ge(s["rw_copied"], RC0 + b * ROUNDS + i)
                    expert_weights(b, i)
                    gate_up(b, i * 2, (i, 0))
                    gate_up(b, i * 2 + 1, (i, 1))
                    down(b, i * 2, (i, 0))
                    down(b, i * 2 + 1, (i, 1))

            parts = {"F1": embed, "F2": hn_transposed, "F3": in_proj, "F6": x_proj, "F7": dt_proj,
                     "T2": out_proj, "T4": h1_transposed, "T5": router, "T7": weights_transposed,
                     "G": gate_up, "D": down}
            pe.wait_ge(s["w_in"], W_ALL)
            pe.wait_ge(s["ones_set"], 1)
            pe.wait_ge(s["zeros_set"], 1)
            pe.wait_ge(s["sel_ready"], 1)
            images.engine = pe
            images(lambda: front_only(parts), scan, parts, moe_alone)

        @block.scalar
        def _(act):
            def norm_affine(b):
                act.wait_ge(s["hnT_done"], b + 1)
                for k in range(2):
                    act.activation(hnT[:, k, :], pD[0:EK, 1, k * T:(k + 1) * T], ACT.Identity,
                                   bias=lnb[:, k:k + 1], scale=lnw[:, k:k + 1]).then_inc(s["hnT_ready"], 1)

            def take_xz(b):
                act.wait_ge(s["in_done"], b * 3 + 1)
                for c in range(2):
                    act.activation(xpad[:, c, CONV - 1:], pBC[0][:, c * T:(c + 1) * T], ACT.Copy).then_inc(s["xc_copied"], 1)
                act.wait_ge(s["in_done"], b * 3 + 2)
                act.activation(xpad[:, 2, CONV - 1:], pD[:, 0, 0:T], ACT.Copy).then_inc(s["xc_copied"], 1)
                act.activation(zth[:, 0, :], pD[:, 0, T:2 * T], ACT.Tanh, scale=0.5).then_inc(s["z_tanh"], 1)
                act.wait_ge(s["in_done"], b * 3 + 3)
                act.activation(zth[:, 1:3, :], pair(pD[:, 1, :]), ACT.Tanh, scale=0.5).then_inc(s["z_tanh"], 1)

            def conv_tanh(b):
                act.wait_ge(s["conv_ready"], b * 3 + 3)
                act.activation(cth[:, :, :], cacc[:, :, :], ACT.Tanh, scale=0.5).then_inc(s["conv_tanh"], 1)

            def take_dtr(b):
                act.wait_ge(s["xp_done"], b * 3 + 1)
                act.activation(dtr[:, :], pD[0:R, 1, 0:T], ACT.Copy).then_inc(s["dtr_ready"], 1)

            def soft_exp(b):
                act.wait_ge(s["dtp_done"], b + 1)
                for c in range(NC):
                    act.activation(vabs[:, c, :], pD[:, c // 2, (c % 2) * T:(c % 2) * T + T], ACT.Abs,
                                   bias=dtb[:, c:c + 1]).then_inc(s["vabs_ready"], 1)
                act.wait_ge(s["vabs_ready"], b * 3 + 3)
                act.activation(vexp[:, :, :], vabs[:, :, :], ACT.Exp, scale=-1.0).then_inc(s["vexp_ready"], 1)

            def decay(b, i, j, r):
                for c in range(NC):
                    v = b * (ROUNDS * SUB) + i * SUB + (j * 3 + c)
                    act.wait_ge(s["scan_done"], 1 + v)
                    for e in range(2):
                        act.activation(da[:, r * SUB + j * 3 + c, e, 1:T], dt[:, c, 1:T], ACT.Exp,
                                       scale=aneg[:, c, bass.ds(i * 4 + j * 2 + e, 1)]).then_inc(s["da_ready"], 1)

            def copy_c(b, i, j, r):
                k = b * PAIRS + i * 2 + j
                act.wait_ge(s["c_filled"], 1 + k)
                act.wait_ge(s["hc_done"], 3 + k * 3)
                act.activation(cbc[:, r * 2 + j, :, :], pair(pBC[1 - j]), ACT.Copy).then_inc(s["c_copied"], 1)

            def copy_weights(b, i):
                act.wait_ge(s["rw_filled"], b * ROUNDS + i + 1)
                act.activation(rwb[:, bass.ds(i * 2, 2), :], pair(pBC[1]), ACT.Copy).then_inc(s["rw_copied"], 1)

            def gate_tanh(b, k, slot=None):
                slot = k % 2 if slot is None else slot
                act.wait_ge(s["gu_done"], GU0 + 1 + b * PAIRS + k)
                act.activation(gth[:, slot, :], pG[:, 0:T], ACT.Tanh, scale=0.5).then_inc(s["g_tanh"], 1)

            def scan(b, moe):
                act.wait_ge(s["u_ready"], b + 1)
                if moe:
                    act.wait_ge(s["hm_ready"], HM0 + (b - 1) * PAIRS)
                with act.Fori(0, ROUNDS // 2) as i2:
                    for r in range(2):
                        i = i2 * 2 + r
                        decay(b, i, 0, r)
                        copy_c(b, i, 0, r)
                        if moe:
                            copy_weights(b - 1, i)
                            if PER_ROUND == 2:
                                gate_tanh(b - 1, i * 2, 0)
                            else:
                                gate_tanh(b - 1, i, r)
                        decay(b, i, 1, r)
                        copy_c(b, i, 1, r)
                        if moe and PER_ROUND == 2:
                            gate_tanh(b - 1, i * 2 + 1, 1)

            def take_h1T(b):
                act.wait_ge(s["h1T_done"], b + 1)
                act.activation(h1Tn[:, :, :], pair(pY[0:EK, 0, :]), ACT.Copy).then_inc(s["h1T_ready"], 1)

            def router_exp(b):
                act.wait_ge(s["logit_ready"], b + 1)
                act.wait_ge(s["nmax_ready"], b + 1)
                for t in range(2):
                    act.activation(lexp[:, t, :], logit[:, t, :], ACT.Exp,
                                   bias=nmax[:, t:t + 1]).then_inc(s["lexp_ready"], 1)

            def commit(b):
                act.wait_ge(s["rwn_ready"], b + 1)
                if not isinstance(b, int) or b > 0:
                    act.wait_ge(s["out_ready"], b * 2)
                for new, old in ((h1n, h1), (h1Tn, h1T), (rw_new, rw_split)):
                    act.activation(old[:, :, :], new[:, :, :], ACT.Copy).then_inc(s["committed"], 1)

            def moe_alone(b):
                act.wait_ge(s["hm_ready"], HM0 + b * PAIRS)
                with act.Fori(0, ROUNDS) as i:
                    copy_weights(b, i)
                    for j in range(2):
                        gate_tanh(b, i * 2 + j, j)

            parts = {"F2": norm_affine, "F3": take_xz, "F4": conv_tanh, "F6": take_dtr,
                     "F7": soft_exp, "T5": take_h1T, "T6": router_exp, "commit": commit,
                     "H": gate_tanh}
            act.wait_ge(s["w_in"], W_ALL)
            act.activation(alog[:, :, :], alog[:, :, :], ACT.Exp).then_inc(s["a_exp"], 1)
            act.wait_ge(s["a_exp"], 1)
            act.mul(aneg[:, :, :], alog[:, :, :], -1.0).then_inc(s["a_ready"], 1)
            act.wait_ge(s["a_ready"], 1)
            act.wait_ge(s["da_reset"], 1)
            images.engine = act
            images(lambda: front_only(parts), scan, parts, moe_alone)

        @block.vector
        def _(dve):
            class Steps:

                def __init__(self, name, per):
                    self.sem, self.per, self.n = s[name], per, 0

                def begin(self, b):
                    self.base, self.n = b * self.per, 0

                def done(self, ins):
                    ins.then_inc(self.sem, 1)
                    self.n += 1

                def wait(self):
                    dve.wait_ge(self.sem, self.base + self.n)

                def end(self):
                    assert self.n == self.per, (self.n, self.per)

            NORM = 2 * 2 + 3 + 3 * NEWTON
            f = Steps("front_v", NORM + 1 + 9 + 1 + 8 + 3 + 1 + DEG + 1)
            w = Steps("tail_v", 1 + NORM + 2 + 2 + 1 + 2 + 1 + 4)
            e = Steps("finish_v", 1 + NORM)

            def settle():
                dve.sem_inc(s["settled"], 1)

            def norm(kind, src, dst, st, ready):
                r, nw, v = rstd[kind], newton[kind], var[kind]
                for t in range(2):
                    st.done(dve.bn_stats(stats[kind][:, t, :], src[:, t, :]))
                st.wait()
                settle()
                for t in range(2):
                    st.done(dve.bn_aggr(mv[kind][:, t, :], stats[kind][:, t, :]))
                st.wait()
                st.done(dve.tensor_scalar(v[:, :], mv[kind][:, :, 1], EPS, None, ALU.add))
                st.wait()
                st.done(dve.tensor_single_scalar(r[:, :].bitcast(I32), v[:, :].bitcast(I32), 1, ALU.logical_shift_right))
                st.wait()
                st.done(dve.tensor_scalar(r[:, :].bitcast(I32), r[:, :].bitcast(I32), -1.0, RSQRT_MAGIC, ALU.mult, ALU.add))
                for _ in range(NEWTON):
                    st.wait()
                    st.done(dve.tensor_tensor(nw[:, :], r[:, :], r[:, :], ALU.mult))
                    st.wait()
                    st.done(dve.scalar_tensor_tensor(nw[:, :], nw[:, :], -0.5, v[:, :], ALU.mult, ALU.mult))
                    st.wait()
                    st.done(dve.scalar_tensor_tensor(r[:, :], nw[:, :], 1.5, r[:, :], ALU.add, ALU.mult))
                st.wait()
                for t in range(2):
                    dve.tensor_scalar(dst[:, t, :], src[:, t, :], mv[kind][:, t, 0:1], r[:, t:t + 1],
                                      ALU.subtract, ALU.mult).then_inc(s[ready], 1)

            def split3(parts, rest, src, st):
                st.done(dve.tensor_copy(parts[0:96], src))
                st.wait()
                st.done(dve.tensor_tensor(rest[0:96], src, parts[0:96], ALU.subtract))
                st.wait()
                st.done(dve.tensor_copy(parts[32:64], rest[32:64]))
                st.done(dve.tensor_copy(parts[64:96], rest[64:96]))
                st.wait()
                return dve.tensor_tensor(parts[64:96], rest[64:96], parts[64:96], ALU.subtract)

            def take_h(b):
                f.begin(b)
                dve.wait_ge(s["embed_done"], b + 1)
                f.done(dve.tensor_copy(h[:, :, :], pair(pD[0:TT, 0, :])))
                f.wait()
                norm("front", h, hn, f, "hn_ready")

            def gate_conv(b):
                dve.wait_ge(s["z_tanh"], b * 2 + 1)
                dve.scalar_tensor_tensor(gate[:, 0, :], zth[:, 0, :], 1.0, pD[:, 0, T:2 * T], ALU.add,
                                         ALU.mult).then_inc(s["gate_ready"], 1)
                dve.wait_ge(s["z_tanh"], b * 2 + 2)
                for c in (1, 2):
                    dve.scalar_tensor_tensor(gate[:, c, :], zth[:, c, :], 1.0, pD[:, 1, (c - 1) * T:c * T], ALU.add,
                                             ALU.mult).then_inc(s["gate_ready"], 1)
                dve.wait_ge(s["xc_copied"], b * 3 + 3)
                for k in range(CONV):
                    for c in range(NC):
                        tap, wk = xpad[:, c, k:k + T], convw[:, c, k:k + 1]
                        if k == 0:
                            ins = dve.tensor_scalar(cacc[:, c, :], tap, wk, convb[:, c:c + 1], ALU.mult, ALU.add)
                        else:
                            ins = dve.scalar_tensor_tensor(cacc[:, c, :], tap, wk, cacc[:, c, :], ALU.mult, ALU.add)
                        if k == CONV - 1:
                            ins.then_inc(s["conv_ready"], 1)
                        else:
                            f.done(ins)
                    if k < CONV - 1:
                        f.wait()

            def silu_conv(b):
                dve.wait_ge(s["conv_tanh"], b + 1)
                f.done(dve.tensor_scalar(cth[:, :, :], cth[:, :, :], 0.5, 0.5, ALU.mult, ALU.add))
                f.wait()
                dve.tensor_tensor(xs[:, :, :], cth[:, :, :], cacc[:, :, :], ALU.mult).then_inc(s["xs_ready"], 1)

            def split_bc(b):
                for q, p in ((0, pBC[0]), (1, pD[:, 0, :])):
                    dve.wait_ge(s["xp_done"], b * 3 + 2 + q)
                    split3(bc_split[:, q], bc_rest[:, q], pair(p[0:96, :]), f).then_inc(s["bc_ready"], 1)

            def softplus(b):
                dve.wait_ge(s["vabs_ready"], b * 3 + 3)
                for c in range(NC):
                    f.done(dve.tensor_scalar(vmax[:, c, :], pD[:, c // 2, (c % 2) * T:(c % 2) * T + T],
                                             dtb[:, c:c + 1], 0.0, ALU.add, ALU.max))
                dve.wait_ge(s["vexp_ready"], b + 1)
                q = LOG1P_Q
                f.done(dve.tensor_scalar(poly[:, :, :], vexp[:, :, :], q[-1], None, ALU.mult))
                for k in range(DEG - 1, -1, -1):
                    f.wait()
                    f.done(dve.scalar_tensor_tensor(poly[:, :, :], poly[:, :, :], q[k], vexp[:, :, :], ALU.add, ALU.mult))
                f.wait()
                f.done(dve.tensor_tensor(dt[:, :, :], poly[:, :, :], vmax[:, :, :], ALU.add))
                f.wait()
                dve.tensor_tensor(u[:, :, :], dt[:, :, :], xs[:, :, :], ALU.mult).then_inc(s["u_ready"], 1)
                f.end()

            def products(b, i, j, c):
                m = j * 3 + c
                v = b * (ROUNDS * SUB) + i * SUB + m
                if c == 0:
                    dve.wait_ge(s["b_filled"], 1 + b * PAIRS + i * 2 + j)
                dve.wait_ge(s["scan_done"], SCAN0 - 1 + v)
                dve.tensor_tensor(pair(pD[:, m % 2, :]), u[:, c:c + 1, :].to_broadcast([128, 2, T]), pair(pBC[j]),
                                  ALU.mult).then_inc(s["dbx_done"], 1)

            def recur(b, i, j, c, r):
                m = j * 3 + c
                v = b * (ROUNDS * SUB) + i * SUB + m
                dve.wait_ge(s["dbx_done"], DBX0 + 1 + v)
                dve.wait_ge(s["da_ready"], 2 + v * 2)
                dve.wait_ge(s["hc_done"], 1 + v)
                dve.tensor_tensor_scan(hs[:, r * SUB + m].rearrange("p a t -> p (a t)"),
                                       da[:, r * SUB + m].rearrange("p a t -> p (a t)"),
                                       pD[:, m % 2, 0:2 * T], 0.0, ALU.mult, ALU.add).then_inc(s["scan_done"], 1)

            def gate_product(b, k, slot=None):
                slot = k % 2 if slot is None else slot
                dve.wait_ge(s["g_tanh"], 1 + b * PAIRS + k)
                dve.scalar_tensor_tensor(hm1[:, slot, :], gth[:, slot, :], 1.0, pG[:, 0:T], ALU.add,
                                         ALU.mult).then_inc(s["hm1_done"], 1)
                dve.wait_ge(s["hm1_done"], 1 + b * PAIRS + k)
                dve.wait_ge(s["hm_ready"], HM0 - 1 + b * PAIRS + k)
                dve.tensor_tensor(hm2[:, slot, :], hm1[:, slot, :], pG[:, 256:256 + T], ALU.mult).then_inc(s["hm2_done"], 1)

            def scan(b, moe):
                dve.wait_ge(s["u_ready"], b + 1)
                settle()
                units = [(j, c) for j in range(2) for c in range(NC)]
                with dve.Fori(0, ROUNDS // 2) as i2:
                    for r in range(2):
                        i = i2 * 2 + r
                        for m, (j, c) in enumerate(units):
                            products(b, i, j, c)
                            if m >= 1:
                                recur(b, i, *units[m - 1], r)
                            if moe and PER_ROUND == 2 and m in (2, 5):
                                gate_product(b - 1, i * 2 + m // 5, m // 5)
                            elif moe and PER_ROUND == 1 and m == 2:
                                gate_product(b - 1, i, r)
                        recur(b, i, *units[-1], r)

            def take_y(b):
                w.begin(b)
                dve.wait_ge(s["y_added"], YA0 + (b + 1) * (ROUNDS * SUB))
                for c in range(NC):
                    dve.scalar_tensor_tensor(yt[:, c, :], xs[:, c, :], dsk[:, c:c + 1], y_of(c), ALU.mult,
                                             ALU.add).then_inc(s["y_taken"], 1)
                dve.wait_ge(s["y_taken"], b * 3 + 3)
                dve.scalar_tensor_tensor(yg[:, :, :], yt[:, :, :], 0.5, gate[:, :, :], ALU.mult,
                                         ALU.mult).then_inc(s["yg_ready"], 1)

            def residual(b):
                dve.wait_ge(s["op_done"], b + 1)
                w.done(dve.scalar_tensor_tensor(res[:, :, :], h[:, :, :], 2.0, pair(pBC[1][0:TT, :]), ALU.mult, ALU.add))
                w.wait()
                norm("tail", res, h1n, w, "h1n_ready")

            def top_8(b):
                dve.wait_ge(s["rt_done"], b + 1)
                dve.tensor_copy(logit[:, :, :], pY[0:TT, 1, 0:128].rearrange("p (t e) -> p t e", t=2)
                                ).then_inc(s["logit_ready"], 1)
                dve.wait_ge(s["logit_ready"], b + 1)
                settle()
                for t in range(2):
                    w.done(dve.max(top8[:, t, :], logit[:, t, :]))
                w.wait()
                dve.tensor_scalar(nmax[:, :], top8[:, :, 0], -1.0, None, ALU.mult).then_inc(s["nmax_ready"], 1)
                for t in range(2):
                    w.done(dve.match_replace(lrest[:, t, :], top8[:, t, :], logit[:, t, :], -3.0e38))
                w.wait()
                w.done(dve.tensor_tensor(lmask[:, :, :], lrest[:, :, :], logit[:, :, :], ALU.not_equal))

            def route(b):
                w.wait()
                dve.wait_ge(s["lexp_ready"], b * 2 + 2)
                for t in range(2):
                    w.done(dve.scalar_tensor_tensor(lmask[:, t, :], lmask[:, t, :], 1.0, lexp[:, t, :], ALU.mult, ALU.mult,
                                                    accum_out=wsum[:, t:t + 1]))
                w.wait()
                w.done(dve.reciprocal(winv[:, :], wsum[:, :]))
                w.wait()
                for t in range(2):
                    dve.tensor_scalar(wrep[:, t],
                                      lmask[:, t, :].rearrange("p (a o e) -> p a o e", a=2, o=1).to_broadcast([TT, 2, 3, HALF]),
                                      winv[:, t:t + 1], 0.5, ALU.mult, ALU.mult).then_inc(s["wrep_ready"], 1)

            def split_weights(b):
                dve.wait_ge(s["wT_done"], b + 1)
                split3(rw_new, rw_rest, pair(pBC[1][0:96, :]), w).then_inc(s["rwn_ready"], 1)
                w.end()

            def finish(b):
                e.begin(b)
                dve.wait_ge(s["dn_done"], DN0 + (b + 1) * PAIRS)
                if not isinstance(b, int) or b > 0:
                    dve.wait_ge(s["stored"], b * 16)
                e.done(dve.tensor_tensor(ores[:, :, :], h1[:, :, :], pair(pM[0:TT, :]), ALU.add))
                e.wait()
                norm("finish", ores, outb, e, "out_ready")
                e.end()

            def moe_alone(b):
                settle()
                with dve.Fori(0, ROUNDS) as i:
                    for j in range(2):
                        gate_product(b, i * 2 + j, j)
                finish(b)

            dve.memset(zero_w[:, :], 0.0)
            dve.memset(zero_x[:, :], 0.0).then_inc(s["zeros_set"], 1)
            dve.memset(ones[:, :], 1.0).then_inc(s["ones_set"], 1)
            dve.memset(xpad[:, :, 0:CONV - 1], 0.0).then_inc(s["pad_set"], 1)
            dve.memset(da[:, :, :, 0:1], 0.0).then_inc(s["da_reset"], 1)
            dve.wait_ge(s["pad_set"], 1)
            dve.wait_ge(s["w_in"], W_ALL)
            dve.tensor_copy(sel_state[:, :, :], eye[:, :].rearrange("p (a o) -> p a o", o=1).to_broadcast([96, HALF, 128]))
            dve.tensor_copy(sel_expert[:, :, :], eye[:, :].rearrange("p (a o) -> p a o", o=1).to_broadcast([96, HALF, 64])
                            ).then_inc(s["sel_ready"], 1)

            parts = {"F1": take_h, "F4": gate_conv, "F5": silu_conv, "F6": split_bc, "F8": softplus,
                     "T1": take_y, "T2": residual, "T6": top_8, "T7": route, "T8": split_weights,
                     "H": gate_product, "finish": finish}
            images.engine = dve
            images(lambda: front_only(parts), scan, parts, moe_alone)

        @block.gpsimd
        def _(pool):
            for name, n in (("dbx_done", DBX0), ("scan_done", SCAN0), ("hc_done", HC0), ("y_added", YA0),
                            ("c_copied", CC0), ("rw_copied", RC0), ("gu_done", GU0), ("dn_done", DN0),
                            ("hm2_done", HM20), ("hm_ready", HM0)):
                pool.sem_inc(s[name], n)

            def weigh(b, k, half=None):
                slot = k % 2 if half is None else half
                at = rwb[:, k, :] if isinstance(k, int) else rwb[:, bass.ds(k, 1), :].rearrange("p a t -> p (a t)")
                pool.wait_ge(s["hm2_done"], HM20 + 1 + b * PAIRS + k)
                pool.wait_ge(s["dn_done"], 1 + b * PAIRS + k)
                pool.tensor_tensor(hm[:, slot, :], hm2[:, slot, :], at, ALU.mult).then_inc(s["hm_ready"], 1)

            def scan(b, moe):
                with pool.Fori(0, ROUNDS // 2) as i2:
                    for r in range(2):
                        i = i2 * 2 + r
                        for j in range(2):
                            pool.wait_ge(s["c_copied"], CC0 + 1 + b * PAIRS + i * 2 + j)
                            for c in range(NC):
                                m = r * SUB + j * 3 + c
                                v = b * (ROUNDS * SUB) + i * SUB + (j * 3 + c)
                                pool.wait_ge(s["scan_done"], SCAN0 + 1 + v)
                                pool.wait_ge(s["y_added"], 1 + v)
                                pool.tensor_tensor(hc[:, m], hs[:, m], cbc[:, r * 2 + j], ALU.mult).then_inc(s["hc_done"], 1)
                            if moe and j == 0:
                                pool.wait_ge(s["rw_copied"], RC0 + (b - 1) * ROUNDS + i + 1)
                            if moe and PER_ROUND == 2:
                                weigh(b - 1, i * 2 + j, j)
                            elif moe and j == 0:
                                weigh(b - 1, i, r)

            def moe_alone(b):
                with pool.Fori(0, ROUNDS) as i:
                    pool.wait_ge(s["rw_copied"], RC0 + b * ROUNDS + i + 1)
                    for j in range(2):
                        weigh(b, i * 2 + j, j)

            images.engine = pool
            images(lambda: None, scan, {"H": weigh}, moe_alone)


LOG1P_Q = log1p_coefficients()


def kernel(**inputs):
    import numpy as np
    import concourse.bacc as bacc
    from concourse import mybir as mb
    from concourse.bass_utils import run_bass_kernel_spmd as run

    a = {k: np.asarray(v) for k, v in inputs.items()}
    p = "L0_attn_"

    def chunks(w, n):
        return w.reshape(n, w.shape[0] // n, *w.shape[1:]).swapaxes(0, 1)

    xp = a[p + "x_proj_w"]
    rows = [xp[:R]] + [xp[R + q * HALF:R + (q + 1) * HALF] for q in range(4) for _ in range(3)]
    gate, up = a["L0_ffn_w_gate"], a["L0_ffn_w_up"]
    gu = np.stack([gate, up]).reshape(2, PAIRS, 2, 2, EK, 64)
    arrays = {
        "x": a["x"].reshape(NB, 3, 8, 16, 8, 16).transpose(0, 3, 5, 1, 2, 4).reshape(NB, 2, 128, T).transpose(0, 2, 1, 3),
        "tok_w": chunks(a["L0_tok_W"], 2),
        "tok_b": a["L0_tok_b"].reshape(1, E),
        "ln_w": a[p + "ln_w"].reshape(2, EK).T,
        "ln_b": a[p + "ln_b"].reshape(2, EK).T,
        "in_w": chunks(a[p + "in_proj_w"].T, 2),
        "conv_w": chunks(a[p + "conv_w"].reshape(NC * 128, CONV), NC),
        "conv_b": a[p + "conv_b"].reshape(NC, 128).T,
        "xp_w": chunks(np.concatenate(rows).T, NC),
        "dtp_w": a[p + "dt_proj_w"].T,
        "dtp_b": a[p + "dt_proj_b"].reshape(NC, 128).T,
        "a_log": chunks(a[p + "A_log"], NC),
        "d_skip": a[p + "D"].reshape(NC, 128).T,
        "out_w": chunks(a[p + "out_proj_w"].T, NC),
        "router_w": chunks(a["L0_ffn_router_w"].T, 2),
        "wgu": gu.transpose(4, 1, 3, 0, 2, 5).reshape(EK, PAIRS, 512),
        "wd": a["L0_ffn_w_down"].reshape(PAIRS, 128, E).transpose(1, 0, 2),
        "ident": np.eye(128, dtype=np.float32),
        "eye3": np.tile(np.eye(HALF, dtype=np.float32), (3, 1)),
    }
    arrays = {k: np.ascontiguousarray(v) for k, v in arrays.items()}
    nc = bacc.Bacc("TRN2", target_bir_lowering=False, num_devices=1)
    aps = {k: nc.dram_tensor(k, v.shape, mb.dt.from_np(v.dtype), kind="ExternalInput").ap() for k, v in arrays.items()}
    out = nc.dram_tensor("out", (NB, T, E), F32, kind="ExternalOutput").ap()
    vit_mamba_moe(nc, out=out, **aps)
    r = run(nc, [arrays], core_ids=[0])
    return r.results[0]["out"]
```

```python
from contextlib import ExitStack

import concourse.bass as bass
from concourse import mybir

F32 = mybir.dt.float32
BF16 = mybir.dt.bfloat16
I32 = mybir.dt.int32
ALU = mybir.AluOpType
ACT = mybir.ActivationFunctionType

NB = 4
T = 192
TT = 96
E = 192
EK = 96
NC = 3
N = 64
R = 12
CONV = 4
PAIRS = 32
HALF = 32
ROUNDS = 16
SHIFT = 4
LOOP_END = 9
RSQRT_MAGIC = float(0x5f3759df)
NEWTON = 3
DEG = 8
SUB = 6
RING = 2 * SUB
EPS = 1e-5


def log1p_coefficients():
    import numpy as np
    at = 0.5 + 0.5 * np.cos(np.pi * (np.arange(DEG + 1) + 0.5) / (DEG + 1))
    cheb = np.polynomial.Chebyshev.fit(at, np.log1p(at) / at, DEG, domain=[0, 1])
    return [float(c) for c in cheb.convert(kind=np.polynomial.Polynomial).coef]


DECAY_FIRST = 1
GATE_AFTER = 1
FRONT_STEPS = {
    (9, 0): ["embed"], (10, 1): ["hn_transposed"], (11, 0): ["norm_affine", "in_proj_01"],
    (11, 1): ["take_xz", "in_proj_2"], (12, 0): ["take_z"], (12, 1): ["conv_tanh"], (13, 0): ["x_proj_dt"],
    (13, 1): ["take_dtr", "dt_proj"], (14, 0): ["soft_exp", "x_proj_bc"], (15, 0): ["keep_bc"]}
TAIL_STEPS = {
    (1, 0): ["out_proj"], (2, 0): ["h1_transposed"], (2, 1): ["take_h1T", "router"],
    (3, 0): ["router_exp", "weights_transposed"], (3, 1): ["keep_rw"]}
KEEP_AFTER = (2, 1)
KEEP_AFTER_0 = (0, 1)
NO_STEPS = ({}, {})
VECTOR_FRONT = {
    (10, 0, 0): ["take_h"], (10, 0, 1): ["front_stats"], (10, 0, 2): ["front_mean"], (10, 1, 0): ["front_rsqrt"],
    (10, 1, 1): ["front_norm"], (12, 0, 1): ["conv_0"], (12, 0, 2): ["conv_1"], (12, 1, 0): ["conv_2"],
    (12, 1, 1): ["conv_3"], (12, 1, 2): ["gate"], (13, 0, 1): ["silu_conv"], (14, 0, 2): ["take_v"],
    (14, 1, 0): ["log1p_a"], (14, 1, 1): ["log1p_b"], (14, 1, 2): ["split_b_head"], (15, 0, 0): ["split_b_rest"],
    (15, 0, 1): ["split_c_head"], (15, 0, 2): ["split_c_rest"], (15, 1, 0): ["log1p_c"]}
FRONT_STEPS_1 = {
    (1, 0): ["embed"], (3, 0): ["hn_transposed"], (3, 1): ["norm_affine"], (4, 0): ["in_proj_01"], (4, 1): ["take_xz"],
    (9, 0): ["in_proj_2"], (9, 1): ["take_z"], (11, 0): ["conv_tanh"], (12, 0): ["x_proj_dt"], (12, 1): ["take_dtr"],
    (13, 0): ["dt_proj"], (13, 1): ["soft_exp"], (14, 0): ["x_proj_bc"], (15, 0): ["keep_bc"]}
VECTOR_FRONT_1 = {
    (2, 0, 0): ["take_h"], (2, 0, 1): ["front_stats"], (2, 0, 2): ["front_mean"], (2, 1, 0): ["front_rsqrt"],
    (2, 1, 1): ["front_norm"], (9, 0, 1): ["conv_0"], (9, 1, 0): ["conv_1"], (9, 1, 2): ["conv_2"],
    (10, 0, 1): ["conv_3"], (10, 1, 1): ["gate"], (11, 1, 1): ["silu_conv"], (14, 0, 0): ["take_v"],
    (14, 0, 2): ["log1p_a"], (14, 1, 1): ["log1p_b"], (14, 1, 2): ["split_b_head"], (15, 0, 0): ["split_b_rest"],
    (15, 0, 1): ["split_c_head"], (15, 0, 2): ["split_c_rest"], (15, 1, 0): ["log1p_c"]}
VECTOR_TAIL = {
    (0, 1, 2): ["take_y"], (1, 1, 1): ["residual"], (1, 1, 2): ["tail_stats"], (2, 0, 0): ["tail_mean"],
    (2, 0, 1): ["tail_rsqrt"], (2, 0, 2): ["tail_norm"], (3, 0, 1): ["top_8"], (3, 0, 2): ["top_8_mask"],
    (3, 1, 0): ["route"], (3, 1, 2): ["split_weights"]}
VECTOR_FINISH = {
    (4, 0, 2): ["take_sum"], (4, 1, 0): ["finish_stats"], (4, 1, 1): ["finish_mean"], (4, 1, 2): ["finish_rsqrt",
    "finish_norm"]}


def vit_mamba_moe(nc, x, tok_w, tok_b, ln_w, ln_b, in_w, conv_w, conv_b, xp_w, dtp_w, dtp_b, a_log, d_skip, out_w,
                  router_w, wgu, wd, ident, eye3, out):
    with ExitStack() as ctx:
        def sb(name, shape, dt=F32):
            return ctx.enter_context(nc.sbuf_tensor(name, shape, dt))

        def bank(name, dt=F32):
            return ctx.enter_context(nc.psum_tensor(name, [128, 512], dt))

        def sem(name):
            return ctx.enter_context(nc.semaphore(name))

        tokw = sb("tokw", [128, 2, E])
        tokb = sb("tokb", [TT, 1, E])
        lnw = sb("lnw", [EK, 2])
        lnb = sb("lnb", [EK, 2])
        inw = sb("inw", [EK, 2, 2 * NC * 128])
        convw = sb("convw", [128, NC, CONV])
        convb = sb("convb", [128, NC])
        xpw = sb("xpw", [128, NC, R + 4 * 96])
        dtw = sb("dtw", [R, NC * 128])
        dtb = sb("dtb", [128, NC])
        alog = sb("alog", [128, NC, N])
        aneg = sb("aneg", [128, NC, N])
        dsk = sb("dsk", [128, NC])
        outw = sb("outw", [128, NC, E])
        rw_w = sb("rw_w", [EK, 2, 64])
        idn = sb("idn", [128, 128])
        eye = sb("eye", [96, HALF])
        sel_state = sb("sel_state", [96, HALF, 128], BF16)
        sel_expert = sb("sel_expert", [96, HALF, 64], BF16)
        zero_w = sb("zero_w", [1, 128], BF16)
        zero_x = sb("zero_x", [1, 2 * T], BF16)

        xb = sb("xb", [128, 2, T])
        h_new = sb("h_new", [TT, 2, E])
        h = sb("h", [TT, 2, E])
        norms = ("front", "tail", "finish")
        stats, mv, var, newton, rstd = ({q: sb(n + q, [TT, 2] + f) for q in norms} for n, f in (
            ("stats_", [6]), ("mv_", [2]), ("var_", []), ("newton_", []), ("rstd_", [])))
        hn = sb("hn", [TT, 2, E])
        hnT = sb("hnT", [EK, 2, T])
        xpad = sb("xpad", [128, NC, CONV - 1 + T])
        zth = sb("zth", [128, NC, T])
        gate_new = sb("gate_new", [128, NC, T])
        gate = sb("gate", [128, NC, T])
        cacc = sb("cacc", [128, NC, T])
        cth = sb("cth", [128, NC, T])
        xs_new = sb("xs_new", [128, NC, T])
        xs = sb("xs", [128, NC, T])
        dtr = sb("dtr", [R, T])
        vabs = sb("vabs", [128, NC, T])
        vexp = sb("vexp", [128, NC, T])
        vmax = sb("vmax", [128, NC, T])
        poly = sb("poly", [128, NC, T])
        dt = sb("dt", [128, NC, T])
        u = sb("u", [128, NC, T])
        bc_new = sb("bc_new", [96, 4, T], BF16)
        bc_split = sb("bc_split", [96, 8, T], BF16)
        bc_rest = sb("bc_rest", [96, 4, T])
        yt = sb("yt", [128, NC, T])
        yg = sb("yg", [128, NC, T])
        res = sb("res", [TT, 2, E])
        h1n = sb("h1n", [TT, 2, E])
        h1Tn = sb("h1Tn", [EK, 2, T])
        h1 = sb("h1", [TT, 2, E])
        h1T = sb("h1T", [EK, 4, T])
        logit = sb("logit", [TT, 2, 64])
        top8 = sb("top8", [TT, 2, 8])
        nmax = sb("nmax", [TT, 2])
        lrest = sb("lrest", [TT, 2, 64])
        lexp = sb("lexp", [TT, 2, 64])
        lmask = sb("lmask", [TT, 2, 64])
        wsum = sb("wsum", [TT, 2])
        winv = sb("winv", [TT, 2])
        wrep = sb("wrep", [TT, 2, 2, 3, HALF])
        rw_new = sb("rw_new", [96, 2, T], BF16)
        rw_split = sb("rw_split", [96, 4, T], BF16)
        rw_rest = sb("rw_rest", [96, 2, T])
        ores = sb("ores", [TT, 2, E])
        outb = sb("outb", [TT, 2, E])

        da = sb("da", [128, RING, 2, T])
        hs = sb("hs", [128, RING, 2, T])
        hc = sb("hc", [128, RING, 2, T])
        bbc = sb("bbc", [128, 4, 2, T])
        cbc = sb("cbc", [128, 4, 2, T])
        dbx = sb("dbx", [128, 2, 2 * T])
        dbx_pool = sb("dbx_pool", [128, 2, 2 * T])
        gu_w = sb("gu_w", [EK, 4, 2, 2, 128])
        dn_w = sb("dn_w", [128, 4, E])
        rwb = sb("rwb", [128, 4, T])
        gth = sb("gth", [128, 2, T])
        hm1 = sb("hm1", [128, 2, T])
        hm2 = sb("hm2", [128, 2, T])
        hm = sb("hm", [128, 2, T])

        pF = [bank("pF0"), bank("pF1")]
        pB, pC = bank("pB"), bank("pC")
        pY = ctx.enter_context(nc.psum_tensor("pY", [128, 2, 512], F32))
        pG = bank("pG")
        pM = bank("pM")

        def y_of(c):
            return pY[:, c // 2, (c % 2) * T:(c % 2) * T + T]

        def pair(ap, w=T):
            return ap[:, 0:2 * w].rearrange("p (a t) -> p a t", a=2)

        names = """w_embed w_in_proj w_x_proj w_tail x_in zeros_set pad_set da_reset a_exp a_ready sel_ready embed_done
            hn_ready hnT_done hnT_ready in_done xc_copied z_tanh gate_ready conv_ready conv_tanh xs_ready xp_done
            dtr_ready bc_ready bc_taken kept dtp_done vabs_ready vexp_ready vmax_ready u_ready b_filled c_filled
            b_copied c_copied dbx_done dbx_pool_done da_ready scan_done hc_done y_added y_taken yg_ready op_done
            h1n_ready h1T_done h1T_ready rt_done logit_ready nmax_ready lexp_ready wrep_ready wT_done rwn_ready
            rw_kept h1T_kept h1_kept sum_taken gu_loaded0 gu_loaded1 gu_loaded2 gu_loaded3 dn_loaded0 dn_loaded1
            dn_loaded2 dn_loaded3 gu_done dn_done rw_filled rw_copied g_tanh hm1_done hm2_done hm_ready out_ready
            stored settled front_v split_v tail_v finish_v""".split()
        s = {n: sem(n) for n in names}

        WEIGHTS = {"w_embed": [(tokw, tok_w), (tokb, tok_b), (idn, ident), (eye, eye3)],
                   "w_in_proj": [(inw, in_w), (lnw, ln_w), (lnb, ln_b), (convw, conv_w), (convb, conv_b)],
                   "w_x_proj": [(xpw, xp_w), (dtw, dtp_w), (dtb, dtp_b), (alog, a_log)],
                   "w_tail": [(outw, out_w), (rw_w, router_w), (dsk, d_skip)]}

        def weights_wait(engine, b, group):
            if isinstance(b, int) and b == 0:
                engine.wait_ge(s[group], 16 * len(WEIGHTS[group]))

        def load_weights(engine, large):
            for group, loads in WEIGHTS.items():
                for n, (dst, src) in enumerate(loads):
                    if (n == 0) == large:
                        engine.dma_start(dst[tuple(slice(None) for _ in dst.shape)], src).then_inc(s[group], 16)

        out_v = out.rearrange("b (t p) e -> p (b t) e", t=2)

        DBX0 = SCAN0 = HC0 = YA0 = RING
        BC0 = CC0 = RC0 = HM20 = 1
        GU0 = DN0 = 4
        HM0, PD0, ST0 = 3, 2, 16

        block = ctx.enter_context(nc.Block())

        class Half:

            def __init__(self, b, i, j, r, scan=True, before=True, moe=True, ahead=True, drain=True, last=False,
                         steps=()):
                self.b, self.i, self.j = b, i, j
                self.r = r
                self.scan = scan
                self.before = before
                self.next = scan and not last
                self.steps = steps
                self.moe = moe
                self.ahead = ahead
                self.drain = drain
                inner = not isinstance(i, int) or i >= SHIFT
                self.mb = b - 1 if inner else b - 2
                self.q = i - SHIFT if inner else i + ROUNDS - SHIFT
                self.k = self.q * 2 + j
                self.rq = (r + SHIFT) % 2
                self.bank = pB if j == 1 and not scan else pG

            def at(self, *where):
                return isinstance(self.i, int) and (self.i, self.j) == where

        def stages(engine, half, parts):
            def step(name, b):
                if name in parts:
                    parts[name](b)

            def head(b, scan=True, tail=True, experts="on", front=NO_STEPS):
                for i in range(SHIFT + 1):
                    for j in range(2):
                        half(Half(b, i, j, i % 2, scan=scan, before=tail if i == 0 else scan,
                                  moe=experts == "on" or (experts == "start" and i == SHIFT),
                                  ahead=experts == "on" or (experts == "start" and i >= SHIFT - 1),
                                  drain=experts == "on",
                                  steps=[(VECTOR_TAIL, b - 1)] * tail + [(VECTOR_FINISH, b - 2)] * (experts == "on") +
                                  [(front[1], b + 1)]))
                        if tail:
                            for name in TAIL_STEPS.get((i, j), ()):
                                step(name, b - 1)
                        for name in front[0].get((i, j), ()):
                            step(name, b + 1)
                        if scan and (i, j) == (KEEP_AFTER if tail else KEEP_AFTER_0):
                            step("keep", b)
                if tail:
                    step("keep_h1", b - 1)
                if experts == "on":
                    step("store", b - 2)

            def rest(b, moe=True, front=(FRONT_STEPS, VECTOR_FRONT)):
                with engine.Fori(0, (LOOP_END - SHIFT - 1) // 2) as turn:
                    for p in range(2):
                        for j in range(2):
                            half(Half(b, turn * 2 + (SHIFT + 1 + p), j, (SHIFT + 1 + p) % 2, moe=moe, ahead=moe,
                                      drain=moe))
                for i in range(LOOP_END, ROUNDS):
                    for j in range(2):
                        half(Half(b, i, j, i % 2, moe=moe, ahead=moe, drain=moe,
                                  last=not front and (i, j) == (ROUNDS - 1, 1),
                                  steps=[(front[1], b + 1)] if front else []))
                        if front:
                            for name in front[0].get((i, j), ()):
                                step(name, b + 1)
                step("flush", b)
                if front:
                    step("dt_u", b + 1)

            def experts_alone(b):
                with engine.Fori(0, ROUNDS // 2 - 1) as turn:
                    for p in range(2):
                        for j in range(2):
                            half(Half(b + 1, turn * 2 + (SHIFT + 1 + p), j, (SHIFT + 1 + p) % 2, scan=False,
                                      before=False))
                for j in range(2):
                    half(Half(b + 1, SHIFT + ROUNDS - 1, j, (SHIFT + 1) % 2, scan=False, before=False, ahead=False))
                step("drain", b)
                for names in VECTOR_FINISH.values():
                    for name in names:
                        step(name, b)
                step("store", b)

            for names in list(FRONT_STEPS.values()) + list(VECTOR_FRONT.values()):
                for name in names:
                    step(name, 0)
            step("dt_u", 0)
            step("first", 0)
            head(0, tail=False, experts="off", front=(FRONT_STEPS_1, VECTOR_FRONT_1))
            rest(0, moe=False, front=(FRONT_STEPS_1, VECTOR_FRONT_1))
            head(1, experts="start")
            with engine.Fori(1, NB - 1) as b:
                rest(b)
                head(b + 1)
            rest(NB - 1, front=None)
            head(NB, scan=False)
            experts_alone(NB - 1)

        class Steps:

            def __init__(self, engine, name, per):
                self.engine, self.sem, self.per, self.n = engine, s[name], per, 0

            def begin(self, b):
                self.base, self.n = b * self.per, 0

            def done(self, ins):
                ins.then_inc(self.sem, 1)
                self.n += 1

            def wait(self):
                self.engine.wait_ge(self.sem, self.base + self.n)

            def end(self):
                assert self.n == self.per, (self.n, self.per)

        def split3_head(engine, parts, rest, src, st):
            st.done(engine.tensor_copy(parts[0:96], src))
            st.wait()
            st.done(engine.tensor_tensor(rest[0:96], src, parts[0:96], ALU.subtract))

        def split3_rest(engine, parts, rest, st):
            st.wait()
            st.done(engine.tensor_copy(parts[32:64], rest[32:64]))
            st.done(engine.tensor_copy(parts[64:96], rest[64:96]))
            st.wait()
            return engine.tensor_tensor(parts[64:96], rest[64:96], parts[64:96], ALU.subtract)

        @block.sync
        def _(sp):
            sp.dma_start(xb[:, :, :], x[0]).then_inc(s["x_in"], 16)
            load_weights(sp, True)

            def load_x(b):
                sp.wait_ge(s["embed_done"], b)
                sp.dma_start(xb[:, :, :].rearrange("p k t -> p (k t)"),
                             x.rearrange("b p k t -> p b (k t)")[:, bass.ds(b, 1), :]).then_inc(s["x_in"], 16)

            def load_experts(b):
                with sp.Fori(0, ROUNDS // 2) as turn:
                    for j in range(4):
                        k = turn * 4 + j
                        sp.wait_ge(s["gu_done"], b * PAIRS + (k + 1))
                        sp.dma_start(gu_w[:, j].rearrange("p k g c -> p (k g c)"),
                                     wgu[:, bass.ds(k, 1), :]).then_inc(s[f"gu_loaded{j}"], 16)
                        sp.wait_ge(s["dn_done"], b * PAIRS + (k + 1))
                        sp.dma_start(dn_w[:, j, :], wd[:, bass.ds(k, 1), :]).then_inc(s[f"dn_loaded{j}"], 16)

            load_x(1)
            with sp.Fori(0, NB - 2) as b:
                load_x(b + 2)
                load_experts(b)
            load_experts(NB - 2)
            load_experts(NB - 1)
            sp.wait_ge(s["stored"], ST0 + 16 * NB)

        @block.tensor
        def _(pe):
            def embed(b):
                weights_wait(pe, b, "w_embed")
                pe.wait_ge(s["x_in"], b * 16 + 16)
                if not isinstance(b, int) or b > 0:
                    pe.wait_ge(s["bc_ready"], b * 2)
                if not isinstance(b, int) or b > 1:
                    pe.wait_ge(s["logit_ready"], b - 1)
                for t in range(2):
                    o = pF[0][0:TT, t * E:(t + 1) * E]
                    for k in range(2):
                        mm = pe.matmul(o, xb[:, k, t * TT:(t + 1) * TT], tokw[:, k, :], start=(k == 0), stop=(k == 1))
                mm.then_inc(s["embed_done"], 1)

            def hn_transposed(b):
                pe.wait_ge(s["hn_ready"], b * 2 + 2)
                if not isinstance(b, int) or b > 1:
                    pe.wait_ge(s["rwn_ready"], b - 1)
                for k in range(2):
                    for t in range(2):
                        mm = pe.transpose(pF[1][0:EK, k * T + t * TT:k * T + (t + 1) * TT],
                                          hn[:, t, k * EK:(k + 1) * EK], idn[0:TT, 0:TT])
                mm.then_inc(s["hnT_done"], 1)

            def in_proj(b, g):
                weights_wait(pe, b, "w_in_proj")
                pe.wait_ge(s["hnT_ready"], b * 2 + 2)
                if g == 2:
                    pe.wait_ge(s["xc_copied"], b * 3 + 2)
                for m in (g * 2, g * 2 + 1):
                    o = pF[g % 2][:, (m % 2) * T:(m % 2) * T + T]
                    for k in range(2):
                        mm = pe.matmul(o, inw[:, k, m * 128:(m + 1) * 128], hnT[:, k, :], start=(k == 0), stop=(k == 1))
                mm.then_inc(s["in_done"], 1)

            def x_proj_dt(b):
                weights_wait(pe, b, "w_x_proj")
                pe.wait_ge(s["xs_ready"], b + 1)
                pe.wait_ge(s["xc_copied"], b * 3 + 3)
                pe.wait_ge(s["gate_ready"], b * 3 + 3)
                for c in range(NC):
                    mm = pe.matmul(pF[1][0:R, 0:T], xpw[:, c, 0:R], xs_new[:, c, :], start=(c == 0), stop=(c == 2))
                mm.then_inc(s["xp_done"], 1)

            def dt_proj(b):
                pe.wait_ge(s["dtr_ready"], b + 1)
                for c in range(NC):
                    o = pF[c // 2][:, (c % 2) * T:(c % 2) * T + T]
                    mm = pe.matmul(o, dtw[:, c * 128:(c + 1) * 128], dtr[:, :], start=True, stop=True)
                mm.then_inc(s["dtp_done"], 1)

            def x_proj_bc(b):
                pe.wait_ge(s["vabs_ready"], b * 3 + 3)
                pe.wait_ge(s["vmax_ready"], b * 3 + 3)
                for q in range(4):
                    o = pF[q // 2][0:96, (q % 2) * T:(q % 2) * T + T]
                    for c in range(NC):
                        mm = pe.matmul(o, xpw[:, c, R + q * 96:R + (q + 1) * 96], xs_new[:, c, :],
                                       start=(c == 0), stop=(c == 2))
                    if q % 2:
                        mm.then_inc(s["xp_done"], 1)

            def fill_b(b, i, j, parity):
                pe.wait_ge(s["b_copied"], BC0 + b * PAIRS + i * 2 + j)
                spread(0, i, j, pB, parity).then_inc(s["b_filled"], 1)

            def fill_c(b, i, j, parity):
                pe.wait_ge(s["c_copied"], CC0 + b * PAIRS + i * 2 + j)
                spread(1, i, j, pC, parity).then_inc(s["c_filled"], 1)

            def spread(which, i, j, bank_, parity):
                for e in range(2):
                    n = i * 4 + j * 2 + e
                    mm = pe.matmul(bank_[:, e * T:(e + 1) * T],
                                   sel_state[:, bass.ds(n % HALF, 1), :].rearrange("p a m -> p (a m)"),
                                   bc_split[:, bass.ds(parity * 4 + which * 2 + n // HALF, 1),
                                            :].rearrange("p a t -> p (a t)"),
                                   start=True, stop=True)
                return mm

            def add_y(b, i, j, r):
                for c in range(NC):
                    v = b * (ROUNDS * SUB) + i * SUB + (j * 3 + c)
                    pe.wait_ge(s["hc_done"], HC0 + 1 + v)
                    for e in range(2):
                        mm = pe.matmul(y_of(c), idn[:, :], hc[:, r * SUB + j * 3 + c, e, :], start=False, stop=False,
                                       skip_group_check=True)
                    mm.then_inc(s["y_added"], 1)

            def zero_y(b):
                if not isinstance(b, int) or b > 0:
                    pe.wait_ge(s["y_taken"], b * 3)
                for k in range(2):
                    pe.matmul(pY[:, k, 0:2 * T], zero_w[:, :], zero_x[:, :], start=True, stop=True)

            def expert_weights(b, q, parity):
                pe.wait_ge(s["rw_kept"], b + 1)
                for j in range(2):
                    ex = q * 4 + j * 2
                    mm = pe.matmul(pC[:, j * T:(j + 1) * T],
                                   sel_expert[:, bass.ds(ex % HALF, 2), :].rearrange("p a m -> p (a m)"),
                                   rw_split[:, bass.ds(parity * 2 + ex // HALF, 1), :].rearrange("p a t -> p (a t)"),
                                   start=True, stop=True)
                mm.then_inc(s["rw_filled"], 1)

            def gate_up(b, q, j, rq, parity, alone=False):
                bank_ = pB if alone and j == 1 else pG
                pe.wait_ge(s["h1T_kept"], b + 1)
                pe.wait_ge(s[f"gu_loaded{rq * 2 + j}"], b * (ROUNDS * 8) + (q - rq) * 8 + 16)
                pe.wait_ge(s["hm2_done"], HM20 + b * PAIRS + q * 2 + j - alone)
                for g in range(2):
                    for c in range(2):
                        mm = pe.matmul(bank_[:, g * 256:g * 256 + T], gu_w[:, rq * 2 + j, c, g, :],
                                       h1T[:, bass.ds(parity * 2 + c, 1), :].rearrange("p a t -> p (a t)"),
                                       start=(c == 0), stop=(c == 1))
                mm.then_inc(s["gu_done"], 1)

            def down(b, q, j, rq):
                pe.wait_ge(s[f"dn_loaded{rq * 2 + j}"], b * (ROUNDS * 8) + (q - rq) * 8 + 16)
                pe.wait_ge(s["hm_ready"], HM0 + 1 + b * PAIRS + q * 2 + j)
                for t in range(2):
                    mm = pe.matmul(pM[0:TT, t * E:(t + 1) * E], hm[:, j, t * TT:(t + 1) * TT], dn_w[:, rq * 2 + j, :],
                                   start=False, stop=False, skip_group_check=True)
                mm.then_inc(s["dn_done"], 1)

            def zero_moe(b):
                if not isinstance(b, int) or b > 0:
                    pe.wait_ge(s["sum_taken"], b)
                pe.matmul(pM[0:TT, 0:2 * E], zero_w[:, 0:TT], zero_x[:, :], start=True, stop=True)

            def next_gate_up(h):
                alone = not h.scan
                if h.j == 0:
                    gate_up(h.mb, h.q, 1, h.rq, h.mb % 2, alone)
                elif h.at(SHIFT - 1, 1):
                    gate_up(h.mb + 1, 0, 0, 0, (h.mb + 1) % 2, alone)
                else:
                    gate_up(h.mb, h.q + 1, 0, 1 - h.rq, h.mb % 2, alone)

            def down_before(h):
                if h.j == 1:
                    down(h.mb, h.q, 0, h.rq)
                elif h.at(SHIFT, 0):
                    down(h.mb - 1, ROUNDS - 1, 1, 1)
                else:
                    down(h.mb, h.q - 1, 1, 1 - h.rq)

            def half(h):
                b, i, j = h.b, h.i, h.j
                if j == 0:
                    after = (b, i, 1, b % 2)
                elif h.at(ROUNDS - 1, 1):
                    after = (b + 1, 0, 0, (b + 1) % 2)
                else:
                    after = (b, i + 1, 0, b % 2)
                if h.next and not h.at(ROUNDS - 1, 1):
                    fill_b(*after)
                if h.moe and j == 0:
                    if h.scan:
                        pe.wait_ge(s["c_copied"], CC0 + 1 + b * PAIRS + i * 2)
                    else:
                        pe.wait_ge(s["rw_copied"], RC0 + h.mb * ROUNDS + h.q)
                    expert_weights(h.mb, h.q, h.mb % 2)
                if h.scan and h.at(1, 0):
                    zero_y(b)
                if h.before:
                    if isinstance(i, int) and i == 0:
                        add_y(b - 1, ROUNDS - 1, j, 1)
                    else:
                        add_y(b, i - 1, j, 1 - h.r)
                if h.next:
                    if h.at(ROUNDS - 1, 1):
                        pe.wait_ge(s["bc_taken"], b + 2)
                        fill_b(*after)
                    if h.moe and j == 0:
                        pe.wait_ge(s["rw_copied"], RC0 + 1 + h.mb * ROUNDS + h.q)
                    fill_c(*after)
                gate_up_next = h.moe if j == 0 else h.ahead
                if gate_up_next and not h.scan:
                    next_gate_up(h)
                if h.moe and h.at(SHIFT, 1):
                    zero_moe(h.mb)
                if (h.drain and j == 0) or (h.moe and j == 1):
                    down_before(h)
                if gate_up_next and h.scan:
                    next_gate_up(h)

            def first_bc(b):
                pe.wait_ge(s["sel_ready"], 2)
                pe.wait_ge(s["bc_taken"], b + 1)
                fill_b(b, 0, 0, 0)
                fill_c(b, 0, 0, 0)

            def out_proj(b):
                weights_wait(pe, b, "w_tail")
                pe.wait_ge(s["yg_ready"], b + 1)
                if not isinstance(b, int) or b < NB - 1:
                    pe.wait_ge(s["bc_ready"], b * 2 + 4)
                for t in range(2):
                    for c in range(NC):
                        mm = pe.matmul(pF[0][0:TT, t * E:(t + 1) * E], yg[:, c, t * TT:(t + 1) * TT], outw[:, c, :],
                                       start=(c == 0), stop=(c == 2))
                mm.then_inc(s["op_done"], 1)

            def h1_transposed(b):
                pe.wait_ge(s["h1n_ready"], b * 2 + 2)
                for k in range(2):
                    for t in range(2):
                        mm = pe.transpose(pF[1][0:EK, k * T + t * TT:k * T + (t + 1) * TT],
                                          h1n[:, t, k * EK:(k + 1) * EK], idn[0:TT, 0:TT])
                mm.then_inc(s["h1T_done"], 1)

            def router(b):
                pe.wait_ge(s["h1T_ready"], b + 1)
                for t in range(2):
                    for k in range(2):
                        mm = pe.matmul(pF[0][0:TT, t * 64:(t + 1) * 64], h1Tn[:, k, t * TT:(t + 1) * TT], rw_w[:, k, :],
                                       start=(k == 0), stop=(k == 1))
                mm.then_inc(s["rt_done"], 1)

            def weights_transposed(b):
                pe.wait_ge(s["wrep_ready"], b * 2 + 2)
                for hf in range(2):
                    for t in range(2):
                        mm = pe.transpose(pF[1][0:96, hf * T + t * TT:hf * T + (t + 1) * TT],
                                          wrep[:, t, hf].rearrange("p s e -> p (s e)"), idn[0:TT, 0:TT])
                mm.then_inc(s["wT_done"], 1)

            def in_proj_01(b):
                in_proj(b, 0)
                in_proj(b, 1)

            def in_proj_2(b):
                in_proj(b, 2)

            def drain(b):
                down(b, ROUNDS - 1, 1, 1)

            parts = {"embed": embed, "hn_transposed": hn_transposed, "in_proj_01": in_proj_01, "in_proj_2": in_proj_2,
                     "x_proj_dt": x_proj_dt, "dt_proj": dt_proj, "x_proj_bc": x_proj_bc, "out_proj": out_proj,
                     "h1_transposed": h1_transposed, "router": router, "weights_transposed": weights_transposed,
                     "drain": drain, "first": first_bc}
            pe.wait_ge(s["zeros_set"], 1)
            stages(pe, half, parts)

        @block.scalar
        def _(act):
            def norm_affine(b):
                weights_wait(act, b, "w_in_proj")
                act.wait_ge(s["hnT_done"], b + 1)
                for k in range(2):
                    act.activation(hnT[:, k, :], pF[1][0:EK, k * T:(k + 1) * T], ACT.Identity,
                                   bias=lnb[:, k:k + 1], scale=lnw[:, k:k + 1]).then_inc(s["hnT_ready"], 1)

            def take_xz(b):
                act.wait_ge(s["in_done"], b * 3 + 1)
                for c in range(2):
                    act.activation(xpad[:, c, CONV - 1:], pF[0][:, c * T:(c + 1) * T],
                                   ACT.Copy).then_inc(s["xc_copied"], 1)
                act.wait_ge(s["in_done"], b * 3 + 2)
                act.activation(xpad[:, 2, CONV - 1:], pF[1][:, 0:T], ACT.Copy).then_inc(s["xc_copied"], 1)
                act.activation(zth[:, 0, :], pF[1][:, T:2 * T], ACT.Tanh, scale=0.5).then_inc(s["z_tanh"], 1)

            def take_z(b):
                act.wait_ge(s["in_done"], b * 3 + 3)
                act.activation(zth[:, 1:3, :], pair(pF[0]), ACT.Tanh, scale=0.5).then_inc(s["z_tanh"], 1)

            def conv_tanh(b):
                act.wait_ge(s["conv_ready"], b * 3 + 3)
                act.activation(cth[:, :, :], cacc[:, :, :], ACT.Tanh, scale=0.5).then_inc(s["conv_tanh"], 1)

            def take_dtr(b):
                act.wait_ge(s["xp_done"], b * 3 + 1)
                act.activation(dtr[:, :], pF[1][0:R, 0:T], ACT.Copy).then_inc(s["dtr_ready"], 1)

            def soft_exp(b):
                weights_wait(act, b, "w_x_proj")
                act.wait_ge(s["dtp_done"], b + 1)
                for c in range(NC):
                    act.activation(vabs[:, c, :], pF[c // 2][:, (c % 2) * T:(c % 2) * T + T], ACT.Abs,
                                   bias=dtb[:, c:c + 1]).then_inc(s["vabs_ready"], 1)
                act.wait_ge(s["vabs_ready"], b * 3 + 3)
                act.activation(vexp[:, :, :], vabs[:, :, :], ACT.Exp, scale=-1.0).then_inc(s["vexp_ready"], 1)

            def decay(b, i, j, r, c):
                v = b * (ROUNDS * SUB) + i * SUB + (j * 3 + c)
                act.wait_ge(s["scan_done"], 1 + v)
                for e in range(2):
                    act.activation(da[:, r * SUB + j * 3 + c, e, 1:T], dt[:, c, 1:T], ACT.Exp,
                                   scale=aneg[:, c, bass.ds(i * 4 + j * 2 + e, 1)]).then_inc(s["da_ready"], 1)

            def copy_b(b, i, j, r):
                k = b * PAIRS + i * 2 + j
                act.wait_ge(s["b_filled"], 1 + k)
                act.wait_ge(s["dbx_done"], DBX0 + (b * ROUNDS + i - 2) * (SUB - 1) + (3, 5)[j])
                if j == 1:
                    act.wait_ge(s["dbx_pool_done"], PD0 + b * ROUNDS + i - 1)
                act.activation(bbc[:, r * 2 + j, :, :], pair(pB), ACT.Copy).then_inc(s["b_copied"], 1)

            def copy_c(b, i, j, r):
                k = b * PAIRS + i * 2 + j
                act.wait_ge(s["c_filled"], 1 + k)
                act.wait_ge(s["hc_done"], 3 + k * 3)
                act.activation(cbc[:, r * 2 + j, :, :], pair(pC), ACT.Copy).then_inc(s["c_copied"], 1)

            def copy_weights(b, q, rq):
                act.wait_ge(s["rw_filled"], b * ROUNDS + q + 1)
                act.wait_ge(s["hm_ready"], HM0 - 2 + b * PAIRS + q * 2)
                act.activation(rwb[:, rq * 2:rq * 2 + 2, :], pair(pC), ACT.Copy).then_inc(s["rw_copied"], 1)

            def gate_tanh(b, k, j, bank_):
                act.wait_ge(s["gu_done"], GU0 + 1 + b * PAIRS + k)
                act.activation(gth[:, j, :], bank_[:, 0:T], ACT.Tanh, scale=0.5).then_inc(s["g_tanh"], 1)

            def decay_next(h, first, end):
                for c in range(first, end):
                    if h.scan and h.j == 0:
                        decay(h.b, h.i, 1, h.r, c)
                    elif h.scan and not h.at(ROUNDS - 1, 1):
                        decay(h.b, h.i + 1, 0, 1 - h.r, c)

            def half(h):
                if h.scan and h.at(0, 0):
                    act.wait_ge(s["u_ready"], h.b + 1)
                    for c in range(NC):
                        decay(h.b, 0, 0, 0, c)
                decay_next(h, 0, DECAY_FIRST)
                if h.moe:
                    if h.j == 0:
                        copy_weights(h.mb, h.q, h.rq)
                    gate_tanh(h.mb, h.k, h.j, h.bank)
                decay_next(h, DECAY_FIRST, NC)
                if h.next:
                    if h.j == 0:
                        copy_bc(h.b, h.i, 1, h.r)
                    elif h.at(ROUNDS - 1, 1):
                        copy_bc(h.b + 1, 0, 0, 0)
                    else:
                        copy_bc(h.b, h.i + 1, 0, 1 - h.r)

            def copy_bc(b, i, j, r):
                copy_b(b, i, j, r)
                copy_c(b, i, j, r)

            def first_a(b):
                act.activation(alog[:, :, :], alog[:, :, :], ACT.Exp).then_inc(s["a_exp"], 1)
                act.wait_ge(s["a_exp"], 1)
                act.mul(aneg[:, :, :], alog[:, :, :], -1.0).then_inc(s["a_ready"], 1)
                act.wait_ge(s["a_ready"], 1)
                act.wait_ge(s["da_reset"], 1)
                copy_bc(0, 0, 0, 0)

            def keep(b):
                act.wait_ge(s["u_ready"], b + 1)
                if not isinstance(b, int) or b > 0:
                    act.wait_ge(s["yg_ready"], b)
                    act.wait_ge(s["h1n_ready"], b * 2)
                for new, old in ((xs_new, xs), (gate_new, gate), (h_new, h)):
                    act.activation(old[:, :, :], new[:, :, :], ACT.Copy).then_inc(s["kept"], 1)

            def keep_bc(b):
                act.wait_ge(s["bc_ready"], b * 2 + 2)
                if not isinstance(b, int) or b > 1:
                    act.wait_ge(s["c_filled"], (b - 1) * PAIRS)
                act.activation(bc_split[:, bass.ds((b % 2) * 4, 4), :], bc_new[:, :, :],
                               ACT.Copy).then_inc(s["bc_taken"], 1)

            def keep_rw(b):
                act.wait_ge(s["rwn_ready"], b + 1)
                if not isinstance(b, int) or b > 0:
                    act.wait_ge(s["rw_copied"], RC0 + (b - 1) * ROUNDS)
                act.activation(rw_split[:, bass.ds((b % 2) * 2, 2), :], rw_new[:, :, :],
                               ACT.Copy).then_inc(s["rw_kept"], 1)

            def keep_h1(b):
                act.wait_ge(s["h1n_ready"], b * 2 + 2)
                if not isinstance(b, int) or b > 0:
                    act.wait_ge(s["sum_taken"], b)
                act.activation(h1[:, :, :], h1n[:, :, :], ACT.Copy).then_inc(s["h1_kept"], 1)

            def take_h1T(b):
                act.wait_ge(s["h1T_done"], b + 1)
                act.activation(h1Tn[:, :, :], pair(pF[1][0:EK, :]), ACT.Copy).then_inc(s["h1T_ready"], 1)
                if not isinstance(b, int) or b > 1:
                    act.wait_ge(s["gu_done"], GU0 + (b - 1) * PAIRS)
                act.activation(h1T[:, bass.ds((b % 2) * 2, 2), :], pair(pF[1][0:EK, :]),
                               ACT.Copy).then_inc(s["h1T_kept"], 1)

            def router_exp(b):
                act.wait_ge(s["logit_ready"], b + 1)
                act.wait_ge(s["nmax_ready"], b + 1)
                for t in range(2):
                    act.activation(lexp[:, t, :], logit[:, t, :], ACT.Exp,
                                   bias=nmax[:, t:t + 1]).then_inc(s["lexp_ready"], 1)

            def store(b):
                act.wait_ge(s["out_ready"], b * 2 + 2)
                act.dma_start(out_v[:, bass.ds(b * 2, 2), :], outb[:, :, :]).then_inc(s["stored"], 16)

            parts = {"first": first_a, "norm_affine": norm_affine, "take_xz": take_xz, "take_z": take_z, "conv_tanh": conv_tanh,
                     "take_dtr": take_dtr, "soft_exp": soft_exp, "keep_bc": keep_bc, "keep": keep, "take_h1T": take_h1T,
                     "router_exp": router_exp, "keep_rw": keep_rw, "keep_h1": keep_h1, "store": store}
            load_weights(act, False)
            stages(act, half, parts)

        @block.vector
        def _(dve):
            NORM = 2 * 2 + 3 + 3 * NEWTON
            front_own = Steps(dve, "front_v", NORM + 1 + 9 + 1 + 1 + DEG + 1)
            split_own = Steps(dve, "split_v", 8)
            tail_own = Steps(dve, "tail_v", 1 + NORM + 2 + 2 + 1 + 2 + 1 + 4)
            finish_own = Steps(dve, "finish_v", NORM)

            def settle():
                dve.sem_inc(s["settled"], 1)

            def norm_stats(kind, src, st):
                st.wait()
                for t in range(2):
                    st.done(dve.bn_stats(stats[kind][:, t, :], src[:, t, :]))

            def norm_mean(kind, st):
                st.wait()
                settle()
                for t in range(2):
                    st.done(dve.bn_aggr(mv[kind][:, t, :], stats[kind][:, t, :]))
                st.wait()
                st.done(dve.tensor_scalar(var[kind][:, :], mv[kind][:, :, 1], EPS, None, ALU.add))

            def norm_rsqrt(kind, st):
                r, nw, v = rstd[kind], newton[kind], var[kind]
                st.wait()
                st.done(dve.tensor_single_scalar(r[:, :].bitcast(I32), v[:, :].bitcast(I32), 1, ALU.logical_shift_right))
                st.wait()
                st.done(dve.tensor_scalar(r[:, :].bitcast(I32), r[:, :].bitcast(I32), -1.0, RSQRT_MAGIC, ALU.mult, ALU.add))
                for _ in range(NEWTON):
                    st.wait()
                    st.done(dve.tensor_tensor(nw[:, :], r[:, :], r[:, :], ALU.mult))
                    st.wait()
                    st.done(dve.scalar_tensor_tensor(nw[:, :], nw[:, :], -0.5, v[:, :], ALU.mult, ALU.mult))
                    st.wait()
                    st.done(dve.scalar_tensor_tensor(r[:, :], nw[:, :], 1.5, r[:, :], ALU.add, ALU.mult))

            def norm_apply(kind, src, dst, st, ready):
                st.wait()
                for t in range(2):
                    dve.tensor_scalar(dst[:, t, :], src[:, t, :], mv[kind][:, t, 0:1], rstd[kind][:, t:t + 1],
                                      ALU.subtract, ALU.mult).then_inc(s[ready], 1)

            def front_stats(b):
                norm_stats("front", h_new, front_own)

            def front_mean(b):
                norm_mean("front", front_own)

            def front_rsqrt(b):
                norm_rsqrt("front", front_own)

            def front_norm(b):
                norm_apply("front", h_new, hn, front_own, "hn_ready")

            def tail_stats(b):
                norm_stats("tail", res, tail_own)

            def tail_mean(b):
                norm_mean("tail", tail_own)

            def tail_rsqrt(b):
                norm_rsqrt("tail", tail_own)

            def tail_norm(b):
                if not isinstance(b, int) or b > 0:
                    dve.wait_ge(s["h1_kept"], b)
                norm_apply("tail", res, h1n, tail_own, "h1n_ready")

            def finish_mean(b):
                norm_mean("finish", finish_own)

            def finish_rsqrt(b):
                norm_rsqrt("finish", finish_own)

            def finish_norm(b):
                dve.wait_ge(s["stored"], ST0 + b * 16)
                norm_apply("finish", ores, outb, finish_own, "out_ready")
                finish_own.end()

            def take_h(b):
                front_own.begin(b)
                weights_wait(dve, b, "w_embed")
                dve.wait_ge(s["embed_done"], b + 1)
                if not isinstance(b, int) or b > 0:
                    dve.wait_ge(s["kept"], b * 3)
                front_own.done(dve.tensor_tensor(h_new[:, :, :], pair(pF[0][0:TT, :]), tokb[:, :, :].to_broadcast([TT, 2, E]),
                                         ALU.add))

            def take_gate(b):
                dve.wait_ge(s["z_tanh"], b * 2 + 1)
                dve.scalar_tensor_tensor(gate_new[:, 0, :], zth[:, 0, :], 1.0, pF[1][:, T:2 * T], ALU.add,
                                         ALU.mult).then_inc(s["gate_ready"], 1)
                dve.wait_ge(s["z_tanh"], b * 2 + 2)
                for c in (1, 2):
                    dve.scalar_tensor_tensor(gate_new[:, c, :], zth[:, c, :], 1.0, pF[0][:, (c - 1) * T:c * T], ALU.add,
                                             ALU.mult).then_inc(s["gate_ready"], 1)

            def conv(b, k):
                if k == 0:
                    weights_wait(dve, b, "w_in_proj")
                    dve.wait_ge(s["pad_set"], 1)
                    dve.wait_ge(s["xc_copied"], b * 3 + 3)
                else:
                    front_own.wait()
                for c in range(NC):
                    tap, wk = xpad[:, c, k:k + T], convw[:, c, k:k + 1]
                    if k == 0:
                        front_own.done(dve.tensor_scalar(cacc[:, c, :], tap, wk, convb[:, c:c + 1], ALU.mult, ALU.add))
                    elif k < CONV - 1:
                        front_own.done(dve.scalar_tensor_tensor(cacc[:, c, :], tap, wk, cacc[:, c, :], ALU.mult, ALU.add))
                    else:
                        dve.scalar_tensor_tensor(cacc[:, c, :], tap, wk, cacc[:, c, :], ALU.mult,
                                                 ALU.add).then_inc(s["conv_ready"], 1)

            def silu_conv(b):
                dve.wait_ge(s["conv_tanh"], b + 1)
                front_own.done(dve.tensor_scalar(cth[:, :, :], cth[:, :, :], 0.5, 0.5, ALU.mult, ALU.add))
                front_own.wait()
                dve.tensor_tensor(xs_new[:, :, :], cth[:, :, :], cacc[:, :, :], ALU.mult).then_inc(s["xs_ready"], 1)

            def take_v(b):
                weights_wait(dve, b, "w_x_proj")
                dve.wait_ge(s["vabs_ready"], b * 3 + 3)
                for c in range(NC):
                    dve.tensor_scalar(vmax[:, c, :], pF[c // 2][:, (c % 2) * T:(c % 2) * T + T],
                                      dtb[:, c:c + 1], 0.0, ALU.add, ALU.max).then_inc(s["vmax_ready"], 1)

            def log1p(b, part):
                if part == 0:
                    dve.wait_ge(s["vexp_ready"], b + 1)
                    front_own.done(dve.tensor_scalar(poly[:, :, :], vexp[:, :, :], LOG1P_Q[-1], None, ALU.mult))
                for k in list(range(DEG - 1, -1, -1))[(0, 2, 5)[part]:(2, 5, 8)[part]]:
                    front_own.wait()
                    front_own.done(dve.scalar_tensor_tensor(poly[:, :, :], poly[:, :, :], LOG1P_Q[k], vexp[:, :, :], ALU.add,
                                                    ALU.mult))

            def split_head(b, q):
                if q == 0:
                    split_own.begin(b)
                    if not isinstance(b, int) or b > 0:
                        dve.wait_ge(s["bc_taken"], b)
                dve.wait_ge(s["xp_done"], b * 3 + 2 + q)
                split3_head(dve, bc_new[:, 2 * q:2 * q + 2], bc_rest[:, 2 * q:2 * q + 2], pair(pF[q][0:96, :]), split_own)

            def split_rest(b, q):
                split3_rest(dve, bc_new[:, 2 * q:2 * q + 2], bc_rest[:, 2 * q:2 * q + 2], split_own).then_inc(s["bc_ready"], 1)

            def flush(b):
                recur(b, ROUNDS - 1, 1, NC - 1, 1)

            def dt_u(b):
                front_own.wait()
                dve.wait_ge(s["vmax_ready"], b * 3 + 3)
                if not isinstance(b, int) or b > 0:
                    dve.wait_ge(s["da_ready"], b * (ROUNDS * SUB * 2))
                    dve.wait_ge(s["dbx_done"], DBX0 + b * (ROUNDS * (SUB - 1)))
                    dve.wait_ge(s["dbx_pool_done"], PD0 + b * ROUNDS)
                front_own.done(dve.tensor_tensor(dt[:, :, :], poly[:, :, :], vmax[:, :, :], ALU.add))
                front_own.wait()
                dve.tensor_tensor(u[:, :, :], dt[:, :, :], xs_new[:, :, :], ALU.mult).then_inc(s["u_ready"], 1)
                front_own.end()

            def products(b, i, j, c, r):
                m = j * 3 + c
                v = b * (ROUNDS * SUB) + i * SUB + m
                slot = r * 2 + j
                if c == 0:
                    dve.wait_ge(s["b_copied"], BC0 + 1 + b * PAIRS + i * 2 + j)
                dve.wait_ge(s["scan_done"], SCAN0 - 1 + v)
                dve.tensor_tensor(pair(dbx[:, m % 2, :]), u[:, c:c + 1, :].to_broadcast([128, 2, T]), bbc[:, slot],
                                  ALU.mult).then_inc(s["dbx_done"], 1)

            def recur(b, i, j, c, r):
                m = j * 3 + c
                v = b * (ROUNDS * SUB) + i * SUB + m
                if m == SUB - 1:
                    product, at = dbx_pool, r
                    dve.wait_ge(s["dbx_pool_done"], PD0 + 1 + b * ROUNDS + i)
                else:
                    product, at = dbx, m % 2
                    dve.wait_ge(s["dbx_done"], DBX0 + 1 + (b * ROUNDS + i) * (SUB - 1) + m)
                dve.wait_ge(s["da_ready"], 2 + v * 2)
                dve.wait_ge(s["hc_done"], 1 + v)
                dve.tensor_tensor_scan(hs[:, r * SUB + m].rearrange("p a t -> p (a t)"),
                                       da[:, r * SUB + m].rearrange("p a t -> p (a t)"),
                                       product[:, at, :], 0.0, ALU.mult, ALU.add).then_inc(s["scan_done"], 1)

            def gate_product(b, k, j, bank_):
                dve.wait_ge(s["g_tanh"], 1 + b * PAIRS + k)
                dve.scalar_tensor_tensor(hm1[:, j, :], gth[:, j, :], 1.0, bank_[:, 0:T], ALU.add,
                                         ALU.mult).then_inc(s["hm1_done"], 1)
                dve.wait_ge(s["hm1_done"], 1 + b * PAIRS + k)
                dve.wait_ge(s["hm_ready"], HM0 - 1 + b * PAIRS + k)
                dve.tensor_tensor(hm2[:, j, :], hm1[:, j, :], bank_[:, 256:256 + T], ALU.mult).then_inc(s["hm2_done"], 1)

            def between(h, c):
                for table, image in h.steps:
                    for name in table.get((h.i, h.j, c), ()):
                        parts[name](image)

            def half(h):
                b, i, j = h.b, h.i, h.j
                if h.scan:
                    if h.at(0, 0):
                        dve.wait_ge(s["u_ready"], b + 1)
                    for c in range(NC):
                        if (j, c) != (1, NC - 1):
                            products(b, i, j, c, h.r)
                        if c > 0:
                            recur(b, i, j, c - 1, h.r)
                        elif j == 1:
                            recur(b, i, 0, NC - 1, h.r)
                        elif not h.at(0, 0):
                            recur(b, i - 1, 1, NC - 1, 1 - h.r)
                        if c == GATE_AFTER and h.moe:
                            gate_product(h.mb, h.k, j, h.bank)
                        between(h, c)
                else:
                    gate_product(h.mb, h.k, j, h.bank)
                    for c in range(NC):
                        between(h, c)

            def take_y(b):
                tail_own.begin(b)
                weights_wait(dve, b, "w_tail")
                dve.wait_ge(s["y_added"], YA0 + (b + 1) * (ROUNDS * SUB))
                dve.wait_ge(s["kept"], b * 3 + 3)
                for c in range(NC):
                    dve.scalar_tensor_tensor(yt[:, c, :], xs[:, c, :], dsk[:, c:c + 1], y_of(c), ALU.mult,
                                             ALU.add).then_inc(s["y_taken"], 1)
                dve.wait_ge(s["y_taken"], b * 3 + 3)
                dve.scalar_tensor_tensor(yg[:, :, :], yt[:, :, :], 0.5, gate[:, :, :], ALU.mult,
                                         ALU.mult).then_inc(s["yg_ready"], 1)

            def residual(b):
                dve.wait_ge(s["op_done"], b + 1)
                tail_own.done(dve.scalar_tensor_tensor(res[:, :, :], h[:, :, :], 2.0, pair(pF[0][0:TT, :]), ALU.mult, ALU.add))

            def top_8(b):
                dve.wait_ge(s["rt_done"], b + 1)
                dve.tensor_copy(logit[:, :, :], pF[0][0:TT, 0:128].rearrange("p (t e) -> p t e", t=2)
                                ).then_inc(s["logit_ready"], 1)
                dve.wait_ge(s["logit_ready"], b + 1)
                settle()
                for t in range(2):
                    tail_own.done(dve.max(top8[:, t, :], logit[:, t, :]))
                tail_own.wait()
                dve.tensor_scalar(nmax[:, :], top8[:, :, 0], -1.0, None, ALU.mult).then_inc(s["nmax_ready"], 1)

            def top_8_mask(b):
                for t in range(2):
                    tail_own.done(dve.match_replace(lrest[:, t, :], top8[:, t, :], logit[:, t, :], -3.0e38))
                tail_own.wait()
                tail_own.done(dve.tensor_tensor(lmask[:, :, :], lrest[:, :, :], logit[:, :, :], ALU.not_equal))

            def route(b):
                tail_own.wait()
                dve.wait_ge(s["lexp_ready"], b * 2 + 2)
                for t in range(2):
                    tail_own.done(dve.scalar_tensor_tensor(lmask[:, t, :], lmask[:, t, :], 1.0, lexp[:, t, :], ALU.mult, ALU.mult,
                                                    accum_out=wsum[:, t:t + 1]))
                tail_own.wait()
                tail_own.done(dve.reciprocal(winv[:, :], wsum[:, :]))
                tail_own.wait()
                for t in range(2):
                    dve.tensor_scalar(wrep[:, t],
                                      lmask[:, t, :].rearrange("p (a o e) -> p a o e", a=2, o=1).to_broadcast([TT, 2, 3, HALF]),
                                      winv[:, t:t + 1], 0.5, ALU.mult, ALU.mult).then_inc(s["wrep_ready"], 1)

            def split_weights(b):
                dve.wait_ge(s["wT_done"], b + 1)
                if not isinstance(b, int) or b > 0:
                    dve.wait_ge(s["rw_kept"], b)
                split3_head(dve, rw_new, rw_rest, pair(pF[1][0:96, :]), tail_own)
                split3_rest(dve, rw_new, rw_rest, tail_own).then_inc(s["rwn_ready"], 1)
                tail_own.end()

            def take_sum(b):
                dve.wait_ge(s["dn_done"], DN0 + (b + 1) * PAIRS)
                dve.wait_ge(s["h1_kept"], b + 1)
                dve.tensor_tensor(ores[:, :, :], h1[:, :, :], pair(pM[0:TT, :]), ALU.add).then_inc(s["sum_taken"], 1)

            def finish_stats(b):
                finish_own.begin(b)
                dve.wait_ge(s["sum_taken"], b + 1)
                for t in range(2):
                    finish_own.done(dve.bn_stats(stats["finish"][:, t, :], ores[:, t, :]))

            dve.memset(zero_w[:, :], 0.0)
            dve.memset(zero_x[:, :], 0.0).then_inc(s["zeros_set"], 1)
            dve.memset(xpad[:, :, 0:CONV - 1], 0.0).then_inc(s["pad_set"], 1)
            dve.memset(da[:, :, :, 0:1], 0.0).then_inc(s["da_reset"], 1)
            dve.wait_ge(s["w_embed"], 16 * len(WEIGHTS["w_embed"]))
            for sel, copies in ((sel_state, 128), (sel_expert, 64)):
                dve.tensor_copy(sel[:, :, :], eye[:, :].rearrange("p (a o) -> p a o", o=1).to_broadcast([96, HALF, copies])
                                ).then_inc(s["sel_ready"], 1)
            parts = {"take_h": take_h, "front_stats": front_stats, "front_mean": front_mean, "front_rsqrt": front_rsqrt,
                     "front_norm": front_norm, "gate": take_gate,
                     "conv_0": lambda b: conv(b, 0), "conv_1": lambda b: conv(b, 1), "conv_2": lambda b: conv(b, 2),
                     "conv_3": lambda b: conv(b, 3), "silu_conv": silu_conv, "take_v": take_v,
                     "log1p_a": lambda b: log1p(b, 0), "log1p_b": lambda b: log1p(b, 1), "log1p_c": lambda b: log1p(b, 2),
                     "split_b_head": lambda b: split_head(b, 0), "split_b_rest": lambda b: split_rest(b, 0),
                     "split_c_head": lambda b: split_head(b, 1), "split_c_rest": lambda b: split_rest(b, 1),
                     "flush": flush, "dt_u": dt_u, "take_y": take_y, "residual": residual, "tail_stats": tail_stats,
                     "tail_mean": tail_mean, "tail_rsqrt": tail_rsqrt, "tail_norm": tail_norm, "top_8": top_8,
                     "top_8_mask": top_8_mask, "route": route, "split_weights": split_weights, "take_sum": take_sum,
                     "finish_stats": finish_stats, "finish_mean": finish_mean, "finish_rsqrt": finish_rsqrt,
                     "finish_norm": finish_norm}
            stages(dve, half, parts)

        @block.gpsimd
        def _(pool):
            for name, n in (("dbx_done", DBX0), ("dbx_pool_done", PD0), ("scan_done", SCAN0), ("hc_done", HC0),
                            ("y_added", YA0), ("b_copied", BC0), ("c_copied", CC0), ("rw_copied", RC0),
                            ("gu_done", GU0), ("dn_done", DN0), ("hm2_done", HM20), ("hm_ready", HM0), ("stored", ST0)):
                pool.sem_inc(s[name], n)

            def weigh(b, k, j, rq):
                pool.wait_ge(s["rw_copied"], RC0 + 1 + b * ROUNDS + (k - j) // 2)
                pool.wait_ge(s["hm2_done"], HM20 + 1 + b * PAIRS + k)
                pool.wait_ge(s["dn_done"], DN0 - 1 + b * PAIRS + k)
                pool.tensor_tensor(hm[:, j, :], hm2[:, j, :], rwb[:, rq * 2 + j, :], ALU.mult).then_inc(s["hm_ready"], 1)

            def half(h):
                b, i, j = h.b, h.i, h.j
                if h.scan and j == 1:
                    v = b * (ROUNDS * SUB) + i * SUB
                    pool.wait_ge(s["u_ready"], b + 1)
                    pool.wait_ge(s["b_copied"], BC0 + 1 + b * PAIRS + i * 2 + 1)
                    pool.wait_ge(s["scan_done"], SCAN0 - SUB + v)
                    pool.tensor_tensor(pair(dbx_pool[:, h.r, :]), u[:, NC - 1:NC, :].to_broadcast([128, 2, T]),
                                       bbc[:, h.r * 2 + 1], ALU.mult).then_inc(s["dbx_pool_done"], 1)
                if h.scan:
                    pool.wait_ge(s["c_copied"], CC0 + 1 + b * PAIRS + i * 2 + j)
                    for c in range(NC):
                        m = h.r * SUB + j * 3 + c
                        v = b * (ROUNDS * SUB) + i * SUB + (j * 3 + c)
                        pool.wait_ge(s["scan_done"], SCAN0 + 1 + v)
                        pool.wait_ge(s["y_added"], 1 + v)
                        pool.tensor_tensor(hc[:, m], hs[:, m], cbc[:, h.r * 2 + j], ALU.mult).then_inc(s["hc_done"], 1)
                if h.moe:
                    weigh(h.mb, h.k, j, h.rq)

            stages(pool, half, {})


LOG1P_Q = log1p_coefficients()


def kernel(**inputs):
    import numpy as np
    import concourse.bacc as bacc
    from concourse import mybir as mb
    from concourse.bass_utils import run_bass_kernel_spmd as run

    a = {k: np.asarray(v) for k, v in inputs.items()}
    p = "L0_attn_"

    def chunks(w, n):
        return w.reshape(n, w.shape[0] // n, *w.shape[1:]).swapaxes(0, 1)

    xp = a[p + "x_proj_w"]
    rows = [xp[:R]] + [xp[R + q * HALF:R + (q + 1) * HALF] for q in range(4) for _ in range(3)]
    gate, up = a["L0_ffn_w_gate"], a["L0_ffn_w_up"]
    gu = np.stack([gate, up]).reshape(2, PAIRS, 2, 2, EK, 64)
    arrays = {
        "x": a["x"].reshape(NB, 3, 8, 16, 8, 16).transpose(0, 3, 5, 1, 2, 4).reshape(NB, 2, 128, T).transpose(0, 2, 1, 3),
        "tok_w": chunks(a["L0_tok_W"], 2),
        "tok_b": np.broadcast_to(a["L0_tok_b"], (TT, 1, E)),
        "ln_w": a[p + "ln_w"].reshape(2, EK).T,
        "ln_b": a[p + "ln_b"].reshape(2, EK).T,
        "in_w": chunks(a[p + "in_proj_w"].T, 2),
        "conv_w": chunks(a[p + "conv_w"].reshape(NC * 128, CONV), NC),
        "conv_b": a[p + "conv_b"].reshape(NC, 128).T,
        "xp_w": chunks(np.concatenate(rows).T, NC),
        "dtp_w": a[p + "dt_proj_w"].T,
        "dtp_b": a[p + "dt_proj_b"].reshape(NC, 128).T,
        "a_log": chunks(a[p + "A_log"], NC),
        "d_skip": a[p + "D"].reshape(NC, 128).T,
        "out_w": chunks(a[p + "out_proj_w"].T, NC),
        "router_w": chunks(a["L0_ffn_router_w"].T, 2),
        "wgu": gu.transpose(4, 1, 3, 0, 2, 5).reshape(EK, PAIRS, 512),
        "wd": a["L0_ffn_w_down"].reshape(PAIRS, 128, E).transpose(1, 0, 2),
        "ident": np.eye(128, dtype=np.float32),
        "eye3": np.tile(np.eye(HALF, dtype=np.float32), (3, 1)),
    }
    arrays = {k: np.ascontiguousarray(v) for k, v in arrays.items()}
    nc = bacc.Bacc("TRN2", target_bir_lowering=False, num_devices=1)
    aps = {k: nc.dram_tensor(k, v.shape, mb.dt.from_np(v.dtype), kind="ExternalInput").ap() for k, v in arrays.items()}
    out = nc.dram_tensor("out", (NB, T, E), F32, kind="ExternalOutput").ap()
    vit_mamba_moe(nc, out=out, **aps)
    r = run(nc, [arrays], core_ids=[0])
    return r.results[0]["out"]
```
